# Optimizing a Trainium2 kernel written in Bass

```python
import numpy as np
import jax
import jax.numpy as jnp

def _softmax(x, axis=-1):
    return jax.nn.softmax(x, axis=axis)

def _gelu(x):
    return jax.nn.gelu(x, approximate=True)

def _silu(x):
    return jax.nn.silu(x)

def _sigmoid(x):
    return jax.nn.sigmoid(x)

def _layernorm(x, axis=-1, eps=1e-05):
    m = jnp.mean(x, axis=axis, keepdims=True)
    v = jnp.var(x, axis=axis, keepdims=True)
    return (x - m) / jnp.sqrt(v + eps)

def _scatter_add(tgt, idx, src, axis=0):
    return tgt.at[idx].add(src)

def _segment_sum(src, seg, n):
    return jax.ops.segment_sum(src, seg, n)
kernel_name = 'mk_macaron_d1_jaxref_r8_4289ad'

def setup_inputs(seed: int=0):
    np.random.seed(seed)
    _w = jnp.asarray

    def _L0_attn_setup():
        import jax, jax.numpy as jnp
        import numpy as np
        B, L, D = (8, 256, 128)
        LEARNED = 32
        WINDOWS = (32.0, 64.0, 128.0, 256.0)

        def _forward(x, Wq, Wk, Wv, Wqkv, bqkv, Wop, W2, b2):
            dt = x.dtype
            Bs, Ls, Ds = x.shape
            windows = jnp.asarray(WINDOWS, dt)
            G = windows.shape[0]
            dh = Ds // G
            BIG = jnp.asarray(1e+18, dt)
            q_in = x @ Wq.T
            _k_unused = x @ Wk.T
            _v_unused = x @ Wv.T
            qkv = (q_in @ Wqkv.T + bqkv).reshape(Bs, Ls, 3, Ds)
            q = qkv[:, :, 0].reshape(Bs, Ls, G, dh)
            k = qkv[:, :, 1].reshape(Bs, Ls, G, dh)
            v = qkv[:, :, 2].reshape(Bs, Ls, G, dh)
            scale = jnp.asarray(1.0 / np.sqrt(Ls), dt)
            scores = jnp.einsum('blgd,bmgd->bglm', q, k) * scale
            h = jax.nn.relu(q_in) @ Wop.T
            dx = jax.nn.sigmoid(h @ W2.T + b2) * Ls
            dx_g = dx[:, None, :, :] + windows[None, :, None, None]
            idx = jnp.arange(Ls)
            dist = jnp.abs(idx[:, None] - idx[None, :]).astype(dt)
            win_mask = jnp.where(idx[None, :] < idx[:, None], BIG, dist)
            masked = jnp.where(win_mask[None, None] > dx_g, -BIG, scores)
            s2 = masked + scores
            attn = jax.nn.softmax(s2, axis=-1)
            out = jnp.einsum('bglm,bmgd->blgd', attn, v).reshape(Bs, Ls, Ds)
            return out
        key = jax.random.key(seed)
        ks = jax.random.split(key, 9)
        s = 0.02
        return {'x': jax.random.normal(ks[0], (B, L, D), jnp.float32), 'Wq': jax.random.normal(ks[1], (D, D), jnp.float32) * s, 'Wk': jax.random.normal(ks[2], (D, D), jnp.float32) * s, 'Wv': jax.random.normal(ks[3], (D, D), jnp.float32) * s, 'Wqkv': jax.random.normal(ks[4], (3 * D, D), jnp.float32) * s, 'bqkv': jnp.zeros((3 * D,), jnp.float32), 'Wop': jax.random.normal(ks[5], (LEARNED, D), jnp.float32) * s, 'W2': jax.random.normal(ks[6], (1, LEARNED), jnp.float32) * s, 'b2': jnp.zeros((1,), jnp.float32)}
    _L0_attn_in = _L0_attn_setup()

    def _L0_ffn_setup():
        import jax, jax.numpy as jnp
        import numpy as np
        DIM = 128
        DEPTH = 6
        HEADS = 16
        DIM_HEAD = 64
        WINDOW = 32
        INNER = HEADS * DIM_HEAD
        DIM_INNER = int(DIM * 4 * 2 / 3)
        QK_SCALE = 8.0

        def shift_tokens(t):
            a, s = jnp.split(t, 2, -1)
            s = jnp.pad(s, ((0, 0), (1, 0), (0, 0)))[:, :-1]
            return jnp.concatenate([a, s], -1)

        def l2norm(t):
            return t / jnp.maximum(jnp.linalg.norm(t, axis=-1, keepdims=True), 1e-12)

        def rotate_half(x):
            x1, x2 = jnp.split(x, 2, -1)
            return jnp.concatenate([-x2, x1], -1)

        def rotary_tables(n):
            half = jnp.arange(0, DIM_HEAD, 2, dtype=jnp.float32)
            inv_freq = 1.0 / 10000.0 ** (half / DIM_HEAD)
            t = jnp.arange(n, dtype=jnp.float32)
            freqs = t[:, None] * inv_freq[None, :]
            freqs = jnp.concatenate([freqs, freqs], -1)
            base_scale = (half + 0.4 * DIM_HEAD) / (1.4 * DIM_HEAD)
            power = (t - n // 2) / (WINDOW // 2)
            scale = base_scale[None, :] ** power[:, None]
            scale = jnp.concatenate([scale, scale], -1)
            return (freqs, scale)

        def local_attention(q, k, v):
            b, h, n, d = q.shape
            w = WINDOW
            nw = n // w
            bq = q.reshape(b, h, nw, w, d)
            bk = k.reshape(b, h, nw, w, d)
            bv = v.reshape(b, h, nw, w, d)

            def look(t):
                p = jnp.pad(t, ((0, 0), (0, 0), (1, 0), (0, 0), (0, 0)))
                return jnp.concatenate([p[:, :, :nw], p[:, :, 1:]], axis=3)
            bk2, bv2 = (look(bk), look(bv))
            seq = jnp.arange(n).reshape(nw, w)
            seq_p = jnp.pad(seq, ((1, 0), (0, 0)), constant_values=-1)
            jt = jnp.concatenate([seq_p[:nw], seq_p[1:]], axis=1)
            it = seq[:, :, None]
            jb = jt[:, None, :]
            mask = (it < jb) | (it > jb + w) | (jb == -1)
            sim = jnp.einsum('bhwie,bhwje->bhwij', bq, bk2) * QK_SCALE
            sim = jnp.where(mask, -jnp.finfo(sim.dtype).max, sim)
            attn = jax.nn.softmax(sim, -1)
            out = jnp.einsum('bhwij,bhwje->bhwie', attn, bv2)
            return out.reshape(b, h, n, d)

        def attn_layer(x, Wqkv, qs, ksc, Wo):
            b, n, _ = x.shape
            qkv = x @ Wqkv
            q, k, v = jnp.split(qkv, 3, -1)
            sh = lambda t: t.reshape(b, n, HEADS, DIM_HEAD).transpose(0, 2, 1, 3)
            q, k, v = (sh(q), sh(k), sh(v))
            q = l2norm(q) * qs
            k = l2norm(k) * ksc
            freqs, scale = rotary_tables(n)
            cos, sin = (jnp.cos(freqs), jnp.sin(freqs))
            q = q * cos * scale + rotate_half(q) * sin * scale
            inv = 1.0 / scale
            k = k * cos * inv + rotate_half(k) * sin * inv
            out = local_attention(q, k, v)
            out = out.transpose(0, 2, 1, 3).reshape(b, n, INNER)
            return out @ Wo

        def ffn_layer(x, g, bln, W1, b1, W2, b2):
            mu = x.mean(-1, keepdims=True)
            var = ((x - mu) ** 2).mean(-1, keepdims=True)
            xn = (x - mu) / jnp.sqrt(var + 1e-05) * g + bln
            hg = xn @ W1 + b1
            a, gate = jnp.split(hg, 2, -1)
            return a * jax.nn.gelu(gate, approximate=False) @ W2 + b2
        key = jax.random.key(seed)
        ks = jax.random.split(key, 8)
        B, N = (2, 256)
        init = lambda k, shape: jax.random.normal(k, shape, jnp.float32) * 0.02
        return {'x': jax.random.normal(ks[0], (B, N, DIM), jnp.float32), 'Wqkv': init(ks[1], (DEPTH, DIM, 3 * INNER)), 'q_scale': jnp.ones((DEPTH, DIM_HEAD), jnp.float32), 'k_scale': jnp.ones((DEPTH, DIM_HEAD), jnp.float32), 'Wo': init(ks[2], (DEPTH, INNER, DIM)), 'ln_g': jnp.ones((DEPTH, DIM), jnp.float32), 'ln_b': jnp.zeros((DEPTH, DIM), jnp.float32), 'W1': init(ks[3], (DEPTH, DIM, 2 * DIM_INNER)), 'b1': jnp.zeros((DEPTH, 2 * DIM_INNER), jnp.float32), 'W2': init(ks[4], (DEPTH, DIM_INNER, DIM)), 'b2': jnp.zeros((DEPTH, DIM), jnp.float32)}
    _L0_ffn_in = _L0_ffn_setup()
    _d = {'L0_attn_x': _L0_attn_in['x'], 'L0_attn_Wq': _L0_attn_in['Wq'], 'L0_attn_Wk': _L0_attn_in['Wk'], 'L0_attn_Wv': _L0_attn_in['Wv'], 'L0_attn_Wqkv': _L0_attn_in['Wqkv'], 'L0_attn_bqkv': _L0_attn_in['bqkv'], 'L0_attn_Wop': _L0_attn_in['Wop'], 'L0_attn_W2': _L0_attn_in['W2'], 'L0_attn_b2': _L0_attn_in['b2'], 'L0_ffn_Wqkv': _L0_ffn_in['Wqkv'], 'L0_ffn_q_scale': _L0_ffn_in['q_scale'], 'L0_ffn_k_scale': _L0_ffn_in['k_scale'], 'L0_ffn_Wo': _L0_ffn_in['Wo'], 'L0_ffn_ln_g': _L0_ffn_in['ln_g'], 'L0_ffn_ln_b': _L0_ffn_in['ln_b'], 'L0_ffn_W1': _L0_ffn_in['W1'], 'L0_ffn_b1': _L0_ffn_in['b1'], 'L0_ffn_W2': _L0_ffn_in['W2'], 'L0_ffn_b2': _L0_ffn_in['b2']}
    _x0 = _d['L0_attn_x']
    _d['L0_attn_x'] = jax.random.normal(jax.random.fold_in(jax.random.key(seed), 1), (1, 2048, 128), dtype=_x0.dtype)
    del _x0
    return _d

def reference(L0_attn_x, L0_attn_Wq, L0_attn_Wk, L0_attn_Wv, L0_attn_Wqkv, L0_attn_bqkv, L0_attn_Wop, L0_attn_W2, L0_attn_b2, L0_ffn_Wqkv, L0_ffn_q_scale, L0_ffn_k_scale, L0_ffn_Wo, L0_ffn_ln_g, L0_ffn_ln_b, L0_ffn_W1, L0_ffn_b1, L0_ffn_W2, L0_ffn_b2):

    def _L0_attn_ref(x, Wq, Wk, Wv, Wqkv, bqkv, Wop, W2, b2):
        import jax, jax.numpy as jnp
        import numpy as np
        B, L, D = (8, 256, 128)
        LEARNED = 32
        WINDOWS = (32.0, 64.0, 128.0, 256.0)

        def _forward(x, Wq, Wk, Wv, Wqkv, bqkv, Wop, W2, b2):
            dt = x.dtype
            Bs, Ls, Ds = x.shape
            windows = jnp.asarray(WINDOWS, dt)
            G = windows.shape[0]
            dh = Ds // G
            BIG = jnp.asarray(1e+18, dt)
            q_in = x @ Wq.T
            _k_unused = x @ Wk.T
            _v_unused = x @ Wv.T
            qkv = (q_in @ Wqkv.T + bqkv).reshape(Bs, Ls, 3, Ds)
            q = qkv[:, :, 0].reshape(Bs, Ls, G, dh)
            k = qkv[:, :, 1].reshape(Bs, Ls, G, dh)
            v = qkv[:, :, 2].reshape(Bs, Ls, G, dh)
            scale = jnp.asarray(1.0 / np.sqrt(Ls), dt)
            scores = jnp.einsum('blgd,bmgd->bglm', q, k) * scale
            h = jax.nn.relu(q_in) @ Wop.T
            dx = jax.nn.sigmoid(h @ W2.T + b2) * Ls
            dx_g = dx[:, None, :, :] + windows[None, :, None, None]
            idx = jnp.arange(Ls)
            dist = jnp.abs(idx[:, None] - idx[None, :]).astype(dt)
            win_mask = jnp.where(idx[None, :] < idx[:, None], BIG, dist)
            masked = jnp.where(win_mask[None, None] > dx_g, -BIG, scores)
            s2 = masked + scores
            attn = jax.nn.softmax(s2, axis=-1)
            out = jnp.einsum('bglm,bmgd->blgd', attn, v).reshape(Bs, Ls, Ds)
            return out
        return _forward(x, Wq, Wk, Wv, Wqkv, bqkv, Wop, W2, b2)

    def _L0_ffn_ref(x, Wqkv, q_scale, k_scale, Wo, ln_g, ln_b, W1, b1, W2, b2):
        import jax, jax.numpy as jnp
        import numpy as np
        DIM = 128
        DEPTH = 6
        HEADS = 16
        DIM_HEAD = 64
        WINDOW = 32
        INNER = HEADS * DIM_HEAD
        DIM_INNER = int(DIM * 4 * 2 / 3)
        QK_SCALE = 8.0

        def shift_tokens(t):
            a, s = jnp.split(t, 2, -1)
            s = jnp.pad(s, ((0, 0), (1, 0), (0, 0)))[:, :-1]
            return jnp.concatenate([a, s], -1)

        def l2norm(t):
            return t / jnp.maximum(jnp.linalg.norm(t, axis=-1, keepdims=True), 1e-12)

        def rotate_half(x):
            x1, x2 = jnp.split(x, 2, -1)
            return jnp.concatenate([-x2, x1], -1)

        def rotary_tables(n):
            half = jnp.arange(0, DIM_HEAD, 2, dtype=jnp.float32)
            inv_freq = 1.0 / 10000.0 ** (half / DIM_HEAD)
            t = jnp.arange(n, dtype=jnp.float32)
            freqs = t[:, None] * inv_freq[None, :]
            freqs = jnp.concatenate([freqs, freqs], -1)
            base_scale = (half + 0.4 * DIM_HEAD) / (1.4 * DIM_HEAD)
            power = (t - n // 2) / (WINDOW // 2)
            scale = base_scale[None, :] ** power[:, None]
            scale = jnp.concatenate([scale, scale], -1)
            return (freqs, scale)

        def local_attention(q, k, v):
            b, h, n, d = q.shape
            w = WINDOW
            nw = n // w
            bq = q.reshape(b, h, nw, w, d)
            bk = k.reshape(b, h, nw, w, d)
            bv = v.reshape(b, h, nw, w, d)

            def look(t):
                p = jnp.pad(t, ((0, 0), (0, 0), (1, 0), (0, 0), (0, 0)))
                return jnp.concatenate([p[:, :, :nw], p[:, :, 1:]], axis=3)
            bk2, bv2 = (look(bk), look(bv))
            seq = jnp.arange(n).reshape(nw, w)
            seq_p = jnp.pad(seq, ((1, 0), (0, 0)), constant_values=-1)
            jt = jnp.concatenate([seq_p[:nw], seq_p[1:]], axis=1)
            it = seq[:, :, None]
            jb = jt[:, None, :]
            mask = (it < jb) | (it > jb + w) | (jb == -1)
            sim = jnp.einsum('bhwie,bhwje->bhwij', bq, bk2) * QK_SCALE
            sim = jnp.where(mask, -jnp.finfo(sim.dtype).max, sim)
            attn = jax.nn.softmax(sim, -1)
            out = jnp.einsum('bhwij,bhwje->bhwie', attn, bv2)
            return out.reshape(b, h, n, d)

        def attn_layer(x, Wqkv, qs, ksc, Wo):
            b, n, _ = x.shape
            qkv = x @ Wqkv
            q, k, v = jnp.split(qkv, 3, -1)
            sh = lambda t: t.reshape(b, n, HEADS, DIM_HEAD).transpose(0, 2, 1, 3)
            q, k, v = (sh(q), sh(k), sh(v))
            q = l2norm(q) * qs
            k = l2norm(k) * ksc
            freqs, scale = rotary_tables(n)
            cos, sin = (jnp.cos(freqs), jnp.sin(freqs))
            q = q * cos * scale + rotate_half(q) * sin * scale
            inv = 1.0 / scale
            k = k * cos * inv + rotate_half(k) * sin * inv
            out = local_attention(q, k, v)
            out = out.transpose(0, 2, 1, 3).reshape(b, n, INNER)
            return out @ Wo

        def ffn_layer(x, g, bln, W1, b1, W2, b2):
            mu = x.mean(-1, keepdims=True)
            var = ((x - mu) ** 2).mean(-1, keepdims=True)
            xn = (x - mu) / jnp.sqrt(var + 1e-05) * g + bln
            hg = xn @ W1 + b1
            a, gate = jnp.split(hg, 2, -1)
            return a * jax.nn.gelu(gate, approximate=False) @ W2 + b2
        for i in range(DEPTH):
            x = attn_layer(shift_tokens(x), Wqkv[i], q_scale[i], k_scale[i], Wo[i]) + x
            x = ffn_layer(shift_tokens(x), ln_g[i], ln_b[i], W1[i], b1[i], W2[i], b2[i]) + x
        return x
    x = L0_attn_x
    x = x + 0.5 * _L0_ffn_ref(_layernorm(x, axis=-1), L0_ffn_Wqkv, L0_ffn_q_scale, L0_ffn_k_scale, L0_ffn_Wo, L0_ffn_ln_g, L0_ffn_ln_b, L0_ffn_W1, L0_ffn_b1, L0_ffn_W2, L0_ffn_b2)
    x = x + _L0_attn_ref(_layernorm(x, axis=-1), L0_attn_Wq, L0_attn_Wk, L0_attn_Wv, L0_attn_Wqkv, L0_attn_bqkv, L0_attn_Wop, L0_attn_W2, L0_attn_b2)
    x = x + 0.5 * _L0_ffn_ref(_layernorm(x, axis=-1), L0_ffn_Wqkv, L0_ffn_q_scale, L0_ffn_k_scale, L0_ffn_Wo, L0_ffn_ln_g, L0_ffn_ln_b, L0_ffn_W1, L0_ffn_b1, L0_ffn_W2, L0_ffn_b2)
    return x

_drawn_inputs = setup_inputs


def setup_inputs(seed=0):
    import zlib

    import numpy as np

    out = dict(_drawn_inputs(seed))
    spreads = {'L0_attn_bqkv': (0.0, 0.1),
     'L0_ffn_q_scale': (1.0, 0.6),
     'L0_ffn_k_scale': (1.0, 0.6),
     'L0_ffn_ln_g': (1.0, 0.6),
     'L0_ffn_ln_b': (0.0, 0.8),
     'L0_ffn_b1': (0.0, 0.8),
     'L0_ffn_b2': (0.0, 0.1)}
    factors = {'L0_attn_Wq': 8.0,
     'L0_attn_Wqkv': 8.0,
     'L0_attn_Wop': 8.0,
     'L0_attn_W2': 8.0,
     'L0_ffn_W1': 3.15,
     'L0_ffn_W2': 3.09}
    for name, (base, spread) in spreads.items():
        noise = np.random.default_rng([zlib.crc32(name.encode()), seed]).standard_normal(out[name].shape)
        drawn = base * np.exp(spread * noise) if base else spread * noise
        out[name] = jnp.asarray(drawn.astype(out[name].dtype))
    for name, factor in factors.items():
        out[name] = (out[name] * factor).astype(out[name].dtype)
    return out
```

```python
from contextlib import ExitStack

import concourse.bass as bass
from concourse import mybir

F32 = mybir.dt.float32
BF16 = mybir.dt.bfloat16
ALU = mybir.AluOpType
ACT = mybir.ActivationFunctionType
AX = mybir.AxisListType.X

P = 128
L = 2048
D = 128
HALF = D // 2
TILES = L // P
DEPTH = 6
HEADS = 16
DH = 64
PAIRS = HEADS // 2
INNER = HEADS * DH
WIN = 32
WINS = P // WIN
SLOTS = 2 * WIN
HID = int(D * 4 * 2 / 3)
HCH = (HID + P - 1) // P
UNITS = DEPTH * TILES
EPS = 1e-5
QK_SCALE = 8.0
NEG = -1e30

LX, LP, LS, LO, LF, LG = 0, 1, 2, 3, 4, 6
ITERS = (UNITS + LG) // 2
FIRST, LAST = LG // 2 + 1, UNITS // 2

GH = 4
GD = D // GH
LEARNED = 32
WINDOWS = (32.0, 64.0, 128.0, 256.0)
BIG = 1e18


class Step:

    def __init__(self, i, j, block, fixed):
        self.i, self.s, self.j, self.base, self.fixed = i, i * 2 + j, j, block * UNITS, fixed

    def on(self, lag):
        return not self.fixed or 0 <= self.s - lag < UNITS

    def unit(self, lag):
        return self.s - lag

    def par(self, lag):
        return (self.j - lag) % 2

    def tile(self, lag):
        return (self.s - lag) % TILES

    def layer(self, lag):
        return (self.s - lag) // TILES

    def count(self, lag, back=0):
        return self.base + (self.s - lag - back + 1)

    def count2(self, lag, back=0):
        return self.i + (self.base // 2 + (self.j - lag - back) // 2 + 1)


def wait(eng, sem, value):
    if isinstance(value, int) and value <= 0:
        return
    eng.wait_ge(sem, value)


def settled(eng, sem):
    eng.wait_ge(sem, 1)


def steps(eng, block, body):
    def both(i, fixed):
        for j in range(2):
            body(Step(i, j, block, fixed))
    for i in range(FIRST):
        both(i, True)
    with eng.Fori(FIRST, LAST) as i:
        both(i, False)
    for i in range(LAST, ITERS):
        both(i, True)


def build(nc, x, fWqkv, fqs, fks, fWo, fg, fb, fW1, fb1, fW2, fb2,
          aWqT, aWqkvT, abqkT, abv, aWopT, aW2T, ab2,
          c_rope, c_decay, c_mask, c_ident, c_dist, out):
    ctx = ExitStack()
    with ctx:
        def sb(name, shape, dt=F32):
            return ctx.enter_context(nc.sbuf_tensor(name, shape, dt))

        def sem(name):
            return ctx.enter_context(nc.semaphore(name))

        x_res = sb("x_res", [P, TILES, D])
        stream = sb("stream", [P, L + 2])
        rope = sb("rope", [P, TILES, 4 * DH])
        qk_gain = sb("qk_gain", [P, DEPTH, 4 * DH])
        mask = sb("mask", [P, TILES, SLOTS], BF16)
        ident = sb("ident", [P, P])
        ident_b = sb("ident_b", [P, P], BF16)
        decay = sb("decay", [P, 1])
        half_pow = sb("half_pow", [P, TILES])
        ln_g = sb("ln_g", [P, DEPTH])
        ln_b = sb("ln_b", [P, DEPTH])
        b2_col = sb("b2_col", [P, DEPTH])
        w_qkv = sb("w_qkv", [P, 2 * 3 * INNER])
        w_o = sb("w_o", [P, 2 * PAIRS * D])
        w_1 = sb("w_1", [P, 2 * 2 * HID])
        w_2 = sb("w_2", [P, 2 * HCH * D])
        b_1 = sb("b_1", [P, 2 * 2 * HID])
        stats = sb("stats", [P, TILES, 6])
        mv = sb("mv", [P, TILES, 2])
        rstd = sb("rstd", [P, TILES])
        ARENA = 28832
        arena = sb("arena", [P, ARENA])

        used = [0]

        def carve(n):
            a = arena[:, used[0]:used[0] + n]
            used[0] += n
            assert used[0] <= ARENA, used[0]
            return a

        v_win = [[carve(2 * PAIRS * DH) for _ in range(WINS)] for _ in range(2)]
        k_bd = carve(PAIRS * 2 * (WIN + P)).rearrange("p (c e t) -> p c e t", c=PAIRS, e=2)
        zeroed = used[0]
        xs = [carve(P) for _ in range(2)]
        xs2 = carve(P)
        table = [carve(4 * DH) for _ in range(2)]
        raw = [carve(INNER) for _ in range(2)]
        ln_scratch = arena[:, used[0] - 2 * INNER:used[0]]
        square = carve(INNER)
        swapped = carve(INNER)
        rot = [carve(INNER) for _ in range(2)]
        q_t = carve(INNER)
        prob = carve(HEADS * SLOTS)
        mask_in = prob.rearrange("p (t k) -> p t k", k=SLOTS)
        prob_t = carve(INNER)
        v_tok = [carve(INNER) for _ in range(2)]
        o_tok = carve(INNER)
        o_t = carve(INNER)
        y1 = carve(D)
        y2 = carve(D)
        xn = carve(D)
        xn_t = carve(D)
        hb = carve(2 * 2 * HID).rearrange("p (b n) -> p b n", b=2)
        gelu = carve(2 * HID).rearrange("p (b n) -> p b n", b=2)
        hid = carve(2 * HCH * P).rearrange("p (b n) -> p b n", b=2)
        hid_t = carve(HCH * P)
        ss = carve(2 * HEADS)
        rn = carve(2 * HEADS)
        smax = carve(HEADS)
        ssum = carve(HEADS)
        rsum = [carve(HEADS) for _ in range(2)]
        st1 = carve(6)
        mv1 = carve(2)
        rs1 = carve(1)
        ve1 = carve(1)

        used[0] = 0
        g_q = carve(GH * L).rearrange("p (h t) -> p h t", h=GH)
        g_k = carve(L)
        g_v = carve(L).rearrange("p (t d) -> p t d", d=D)
        g_dist = carve(L)
        g_s = [carve(L) for _ in range(2)]
        g_mask = carve(L)
        g_pt = [carve(L) for _ in range(2)]
        g_in = carve(L)
        g_relu = g_pt[0]
        g_xt = g_s[0]
        g_h = g_s[1]
        g_w = carve(D + 3 * D + LEARNED + 1)
        g_bqk = carve(2)
        g_bv = carve(D)
        g_b2 = carve(1)
        g_thr = carve(TILES * GH).rearrange("p (t h) -> p t h", h=GH)
        g_dx = carve(TILES)
        g_mx = carve(2 * 4).rearrange("p (b c) -> p b c", b=2)
        g_nm = carve(2)
        g_sum = carve(GH * 2)
        g_rs = carve(GH * 2)
        g_ot = carve(P)

        tgroups, total = [], 0
        for n in range(TILES * GH):
            keys = L - n // GH * P
            tgroups.append([(total + c, min(512, keys - c * 512)) for c in range((keys + 511) // 512)])
            total += len(tgroups[-1])

        def ln_out(n):
            return g_mask if n == 1 else ln_scratch

        A = ctx.enter_context(nc.psum_tensor("ps_a", [P, 1024], F32))
        T = [ctx.enter_context(nc.psum_tensor(f"ps_t{n}", [P, 512], F32)) for n in range(2)]
        S = ctx.enter_context(nc.psum_tensor("ps_s", [P, 1024], F32))
        H = [ctx.enter_context(nc.psum_tensor(f"ps_h{n}", [P, 512], F32)) for n in range(2)]

        def s_bank(k):
            return (A, S)[k // 2 % 2][:, k % 2 * 512:k % 2 * 512 + 512]

        def post_banks(g):
            return (T[0], T[1]) if g % 2 == 0 else (A[:, 0:512], A[:, 512:1024])

        names = """const_in cast_done x_in w_in zero_done misc_done ln_stats ln_mv ln_rstd ln_norm ln_ps ln_lo out_done
            post_ps post_add stream_ready xs_ready table_ready proj_q proj_k proj_v raw_q raw_k sq_q sq_k
            v_ready v_dma0 v_dma1 v_halo0 v_halo1 t1_q t1_k red_q red_k sw_q sw_k add_q add_k rn_q rn_k mx_q mx_k rot_q rot_k
            qt_ps qt_sb kt_ps kt_sb halo scores_ps max_done sub_done exp_done sum_done rsum_done
            pt_ps pt_sb av_ps o_ready ot_ps ot_sb y1_ps y1_sb y1t_ps attn_res
            xs2_ready f1_ps bn_done mv_done ve_done rs_done xn_ready xnt_ps xnt_sb h_ps hb_done gelu_done hid_done
            ht_ps ht_sb y2_ps y2_sb y2t_ps
            g_win g_zero g_qin g_qin_sb g_relu_sb g_qk_ps g_qk_sb g_v_ps g_v_sb g_hps g_hsb g_zps g_zc g_thr_done
            g_sps g_msk g_smx g_mxd g_nmx g_exp g_rsd g_tps g_tev g_tev1 g_ops g_otsb g_ops2 g_upd""".split()
        q = {n: sem(n) for n in names}

        (const_in, cast_done, x_in, w_in, zero_done, misc_done, ln_stats, ln_mv, ln_rstd, ln_norm, ln_ps, ln_lo, out_done,
         post_ps, post_add, stream_ready, xs_ready, table_ready, proj_q, proj_k, proj_v, raw_q, raw_k, sq_q, sq_k,
         v_ready, v_dma0, v_dma1, v_halo0, v_halo1, t1_q, t1_k, red_q, red_k, sw_q, sw_k, add_q, add_k, rn_q, rn_k, mx_q, mx_k,
         rot_q, rot_k, qt_ps, qt_sb, kt_ps, kt_sb, halo, scores_ps, max_done, sub_done, exp_done, sum_done,
         rsum_done, pt_ps, pt_sb, av_ps, o_ready, ot_ps, ot_sb, y1_ps, y1_sb, y1t_ps, attn_res,
         xs2_ready, f1_ps, bn_done, mv_done, ve_done, rs_done, xn_ready, xnt_ps, xnt_sb, h_ps, hb_done, gelu_done,
         hid_done, ht_ps, ht_sb, y2_ps, y2_sb, y2t_ps,
         g_win, g_zero, g_qin, g_qin_sb, g_relu_sb, g_qk_ps, g_qk_sb, g_v_ps, g_v_sb, g_hps, g_hsb, g_zps, g_zc,
         g_thr_done, g_sps, g_msk, g_smx, g_mxd, g_nmx, g_exp, g_rsd, g_tps, g_tev, g_tev1, g_ops, g_otsb, g_ops2,
         g_upd) = (q[n] for n in names)

        v_dma, v_halo = (v_dma0, v_dma1), (v_halo0, v_halo1)
        W_DMAS = 5
        STREAM0 = TILES + UNITS

        def stream_count(step, lag):
            return step.base // UNITS * STREAM0 + step.s - lag + 1

        block = ctx.enter_context(nc.Block())

        @block.sync
        def _(sp):
            for t0 in range(0, TILES, 4):
                sp.dma_start(x_res[:, t0:t0 + 4, :],
                             x[0].rearrange("(t p) d -> p t d", p=P)[:, t0:t0 + 4, :]).then_inc(x_in, 16)
            for dst, src in ((ident[:], c_ident), (rope[:], c_rope), (mask_in, c_mask),
                             (decay[:], c_decay), (ln_g[:], fg), (ln_b[:], fb), (b2_col[:], fb2)):
                sp.dma_start(dst, src).then_inc(const_in, 16)
            gain = qk_gain[:].rearrange("p l (a h d) -> p l a h d", a=4, h=2)
            for a, src in ((0, fqs), (2, fks)):
                row = src.rearrange("l (h d) -> l h d", h=2)
                sp.dma_start(qk_gain[:, :, a * DH:(a + 1) * DH], src.partition_broadcast(P)).then_inc(const_in, 16)
                for h in range(2):
                    sp.dma_start(gain[:, :, a + 1, h, :], row[:, 1 - h, :].partition_broadcast(P))\
                      .then_inc(const_in, 16)

            def load_layer(layer):
                par = layer % 2
                lay = bass.ds(layer, 1)
                sp.dma_start(w_qkv[:, bass.ds(par * 3 * INNER, 3 * INNER)],
                             fWqkv[lay].rearrange("a p n -> p (a n)")).then_inc(w_in, 16)
                sp.dma_start(w_o[:, bass.ds(par * PAIRS * D, PAIRS * D)].rearrange("p (c n) -> p c n", c=PAIRS),
                             fWo[lay].rearrange("a (c p) n -> p (a c) n", p=P)).then_inc(w_in, 16)
                sp.dma_start(w_1[:, bass.ds(par * 2 * HID, 2 * HID)],
                             fW1[lay].rearrange("a p n -> p (a n)")).then_inc(w_in, 16)
                sp.dma_start(w_2[:, bass.ds(par * HCH * D, HCH * D)].rearrange("p (c n) -> p c n", c=HCH),
                             fW2[lay].rearrange("a p c n -> p (a c) n")).then_inc(w_in, 16)
                sp.dma_start(b_1[:, bass.ds(par * 2 * HID, 2 * HID)],
                             fb1[lay].rearrange("a n -> (a n)").partition_broadcast(P)).then_inc(w_in, 16)

            def spread_v(blk, unit, par):
                count = blk * UNITS + unit
                sp.wait_ge(v_ready, count + 1)
                for e in range(2):
                    cols = slice(e * PAIRS * DH, (e + 1) * PAIRS * DH)
                    row = e * SLOTS
                    sp.dma_start(v_win[par][0][row + WIN:row + SLOTS, cols],
                                 v_tok[par][0:WIN, cols]).then_inc(v_dma[par], 16)
                    for w in range(1, WINS):
                        sp.dma_start(v_win[par][w][row:row + SLOTS, cols],
                                     v_tok[par][(w - 1) * WIN:(w + 1) * WIN, cols]).then_inc(v_dma[par], 16)
                wait(sp, av_ps, count)
                for e in range(2):
                    cols = slice(e * PAIRS * DH, (e + 1) * PAIRS * DH)
                    sp.dma_start(v_win[1 - par][0][e * SLOTS:e * SLOTS + WIN, cols],
                                 v_tok[par][P - WIN:P, cols]).then_inc(v_halo[par], 16)

            def stack(blk):
                wait(sp, zero_done, 1 + blk)
                for half in range(2):
                    if half == 0:
                        spread_v(blk, 0, 0)
                        spread_v(blk, 1, 1)
                        with sp.Fori(1, TILES // 4) as k:
                            for j in range(2):
                                spread_v(blk, k * 2 + j, j)
                    else:
                        load_layer(1)
                        with sp.Fori(TILES // 4, TILES // 2) as k:
                            for j in range(2):
                                spread_v(blk, k * 2 + j, j)
                with sp.Fori(1, DEPTH - 1) as layer:
                    with sp.Fori(0, TILES // 4) as k:
                        for j in range(2):
                            spread_v(blk, layer * TILES + k * 2 + j, j)
                    load_layer(layer + 1)
                    with sp.Fori(TILES // 4, TILES // 2) as k:
                        for j in range(2):
                            spread_v(blk, layer * TILES + k * 2 + j, j)
                with sp.Fori((DEPTH - 1) * TILES // 2, DEPTH * TILES // 2) as k:
                    for j in range(2):
                        spread_v(blk, k * 2 + j, j)

            load_layer(0)
            stack(0)
            sp.wait_ge(post_add, 4)
            for dst, src in ((g_dist, c_dist), (g_w[:, 0:D], aWqT), (g_w[:, D:4 * D], aWqkvT),
                             (g_w[:, 4 * D:4 * D + LEARNED], aWopT),
                             (g_w[0:LEARNED, 4 * D + LEARNED:4 * D + LEARNED + 1], aW2T),
                             (g_bqk, abqkT), (g_bv, abv.partition_broadcast(P)), (g_b2, ab2.partition_broadcast(P))):
                sp.dma_start(dst, src).then_inc(g_win, 16)
            load_layer(0)
            stack(1)
            sp.wait_ge(post_add, 8)
            sp.dma_start(out[0].rearrange("(t p) d -> p t d", p=P), x_res[:]).then_inc(out_done, 16)
            sp.wait_ge(out_done, 16)

        @block.gpsimd
        def _(pool):
            pool.memset(half_pow[:], -0.5).then_inc(misc_done, 1)

            def layer_norm_rstd(n):
                pool.wait_ge(ln_mv, n + 1)
                pool.tensor_scalar(rstd[:], mv[:, :, 1], EPS, None, ALU.add).then_inc(ln_rstd, 1)
                pool.wait_ge(ln_rstd, 2 * n + 1)
                pool.tensor_tensor(rstd[:], rstd[:], half_pow[:], ALU.pow).then_inc(ln_rstd, 1)

            def body(st):
                if st.on(LX):
                    if st.fixed and st.s == 0:
                        wait(pool, const_in, 16 * (7 + 6))
                    wait(pool, t1_k, st.count(LX, 2))
                    wait(pool, sw_k, st.count(LX, 2))
                    pool.tensor_tensor(table[st.par(LX)], rope[:, bass.ds(st.tile(LX), 1), :].rearrange("p a n -> p (a n)"),
                                       qk_gain[:, bass.ds(st.layer(LX), 1), :].rearrange("p a n -> p (a n)"),
                                       ALU.mult).then_inc(table_ready, 1)
                def swap_halves(n, raw_s, sw_s, used_s, used):
                    tab = table[st.par(LP)].rearrange("p (a h d) -> p a h d", a=4, h=2)[:, 2 * n + 1]
                    src = raw[n].rearrange("p (c h d) -> p c h d", h=2, d=DH // 2)
                    dst = swapped.rearrange("p (c h d) -> p c h d", h=2, d=DH // 2)
                    wait(pool, used_s, used)
                    pool.wait_ge(table_ready, st.count(LP))
                    pool.wait_ge(raw_s, st.count(LP))
                    for h in range(2):
                        last = pool.tensor_tensor(dst[:, :, h, :], src[:, :, 1 - h, :],
                                                  tab[:, h:h + 1, :].to_broadcast([P, HEADS, DH // 2]), ALU.mult)
                    last.then_inc(sw_s, 1)
                def add_swapped(n, sw_s, t1_s, add_s):
                    pool.wait_ge(sw_s, st.count(LP))
                    pool.wait_ge(t1_s, st.count(LP))
                    pool.tensor_tensor(rot[n], rot[n], swapped, ALU.add).then_inc(add_s, 1)
                def inverse_norm(n, mx_s, rn_s):
                    pool.wait_ge(mx_s, st.count(LP))
                    c = slice(n * HEADS, (n + 1) * HEADS)
                    pool.tensor_tensor(rn[:, c], ss[:, c], half_pow[:, 0:HEADS], ALU.pow).then_inc(rn_s, 1)
                if st.on(LP):
                    swap_halves(0, raw_q, sw_q, add_k, st.count(LP, 1))
                if st.on(LP):
                    add_swapped(0, sw_q, t1_q, add_q)
                if st.on(LF):
                    pool.wait_ge(ve_done, st.count(LF))
                    pool.tensor_tensor(rs1, ve1, half_pow[:, 0:1], ALU.pow).then_inc(rs_done, 1)
                if st.on(LP):
                    inverse_norm(0, mx_q, rn_q)
                    swap_halves(1, raw_k, sw_k, add_q, st.count(LP))
                if st.on(LP):
                    add_swapped(1, sw_k, t1_k, add_k)
                    inverse_norm(1, mx_k, rn_k)

            pool.wait_ge(misc_done, 1)
            layer_norm_rstd(0)
            steps(pool, 0, body)
            layer_norm_rstd(1)
            layer_norm_rstd(2)
            steps(pool, 1, body)

        @block.vector
        def _(dve):
            def zero_blocks(n):
                dve.memset(arena[:, 0:zeroed], 0.0).then_inc(zero_done, 1)

            def layer_norm(n):
                for t in range(TILES):
                    last = dve.bn_stats(stats[:, t, :], x_res[:, t, :])
                last.then_inc(ln_stats, 1)
                dve.wait_ge(ln_stats, n + 1)
                for t in range(TILES):
                    last = dve.bn_aggr(mv[:, t, :], stats[:, t, :])
                last.then_inc(ln_mv, 1)
                dve.wait_ge(ln_rstd, 2 * n + 2)
                dve.wait_ge(ln_mv, n + 1)
                for t in range(TILES):
                    last = dve.tensor_scalar(ln_out(n)[:, t * D:(t + 1) * D], x_res[:, t, :], mv[:, t, 0:1],
                                             rstd[:, t:t + 1], ALU.subtract, ALU.mult)
                last.then_inc(ln_norm, 1)

            def post(n):
                for g in range(4):
                    dve.wait_ge(post_ps, 4 * n + g + 1)
                    for h, bank in enumerate(post_banks(g)):
                        dst = x_res[:, 4 * g:4 * g + 4, h * HALF:(h + 1) * HALF]
                        last = dve.scalar_tensor_tensor(dst, bank[:, 0:4 * HALF].rearrange("p (t d) -> p t d", t=4),
                                                        0.5, dst, ALU.mult, ALU.add)
                    last.then_inc(post_add, 1)
                dve.wait_ge(post_add, 4 * n + 4)
                for par in range(2):
                    dve.wait_ge(v_halo[par], 16 * UNITS * (n + 1))

            def body(st):
                def rotate(n, raw_s, ps_s, sq_s, t1_s, red_s, mx_s):
                    tab = table[st.par(LP)][:, 2 * n * DH:(2 * n + 1) * DH]
                    dve.wait_ge(raw_s, st.count(LP))
                    dve.wait_ge(table_ready, st.count(LP))
                    wait(dve, ps_s, 2 * st.count(LS))
                    dve.tensor_tensor(rot[n].rearrange("p (h d) -> p h d", d=DH),
                                      raw[n].rearrange("p (h d) -> p h d", d=DH),
                                      tab.unsqueeze(1).to_broadcast([P, HEADS, DH]), ALU.mult).then_inc(t1_s, 1)
                    dve.wait_ge(sq_s, st.count(LP))
                    dve.tensor_reduce(ss[:, n * HEADS:(n + 1) * HEADS], square.rearrange("p (h d) -> p h d", d=DH),
                                      AX, ALU.add).then_inc(red_s, 1)
                    dve.wait_ge(red_s, st.count(LP))
                    c = slice(n * HEADS, (n + 1) * HEADS)
                    dve.tensor_scalar(ss[:, c], ss[:, c], 1e-24, None, ALU.max).then_inc(mx_s, 1)
                def normalise(n, add_s, rn_s, rot_s):
                    dve.wait_ge(add_s, st.count(LP))
                    dve.wait_ge(rn_s, st.count(LP))
                    r = rot[n].rearrange("p (h d) -> p h d", d=DH)
                    dve.tensor_tensor(r, r, rn[:, n * HEADS:(n + 1) * HEADS].unsqueeze(2)
                                      .to_broadcast([P, HEADS, DH]), ALU.mult).then_inc(rot_s, 1)
                if st.on(LF):
                    dve.wait_ge(y1t_ps, st.count(LF))
                    t0 = st.tile(LF) * P
                    lo, hi = stream[0:HALF, bass.ds(t0, P)], stream[HALF:P, bass.ds(t0 + 1, P)]
                    dve.tensor_tensor(lo, H[0][0:HALF, 0:P], lo, ALU.add)
                    dve.tensor_tensor(hi, H[0][HALF:P, 0:P], hi, ALU.add).then_inc(attn_res, 1)
                    settled(dve, ln_stats)
                    dve.wait_ge(attn_res, st.count(LF))
                    dve.tensor_copy(xs2, stream[:, bass.ds(t0, P)]).then_inc(xs2_ready, 1)
                if st.on(LP):
                    rotate(0, raw_q, qt_ps, sq_q, t1_q, red_q, mx_q)
                if st.on(LO):
                    dve.wait_ge(av_ps, st.count(LO))
                    dve.wait_ge(rsum_done, st.count(LO))
                    dve.tensor_tensor(o_tok.rearrange("p (h d) -> p h d", d=DH),
                                      S[:].rearrange("p (h d) -> p h d", d=DH),
                                      rsum[st.par(LO)].unsqueeze(2).to_broadcast([P, HEADS, DH]), ALU.mult)\
                       .then_inc(o_ready, 1)
                if st.on(LF):
                    dve.wait_ge(f1_ps, st.count(LF))
                    dve.bn_stats(st1, H[0][:, 0:D]).then_inc(bn_done, 1)
                    settled(dve, ln_stats)
                    dve.wait_ge(bn_done, st.count(LF))
                    dve.bn_aggr(mv1, st1).then_inc(mv_done, 1)
                    dve.wait_ge(mv_done, st.count(LF))
                    wait(dve, rs_done, st.count(LF, 1))
                    dve.tensor_scalar(ve1, mv1[:, 1:2], EPS, None, ALU.add).then_inc(ve_done, 1)
                if st.on(LF):
                    dve.wait_ge(rs_done, st.count(LF))
                    dve.tensor_scalar(xn, H[0][:, 0:D], mv1[:, 0:1], rs1, ALU.subtract, ALU.mult)\
                       .then_inc(xn_ready, 1)
                if st.on(LG) and st.j == 0:
                    n = st.base // 2 + (st.s - LG) // 2 + 1
                    dve.wait_ge(gelu_done, n)
                    wait(dve, ht_ps, st.count(LG, 1))
                    dve.tensor_tensor(hid[:, :, 0:HID], hb[:, :, 0:HID], gelu, ALU.mult).then_inc(hid_done, 1)
                if st.on(LP):
                    rotate(1, raw_k, kt_ps, sq_k, t1_k, red_k, mx_k)
                if st.on(LS):
                    s3 = S[:].rearrange("p (h k) -> p h k", k=SLOTS)
                    dve.wait_ge(scores_ps, st.count(LS))
                    dve.tensor_reduce(smax, s3, AX, ALU.max).then_inc(max_done, 1)
                    dve.wait_ge(max_done, st.count(LS))
                    wait(dve, pt_ps, 2 * st.count(LO))
                    dve.tensor_tensor(prob.rearrange("p (h k) -> p h k", k=SLOTS), s3,
                                      smax.unsqueeze(2).to_broadcast([P, HEADS, SLOTS]), ALU.subtract)\
                       .then_inc(sub_done, 1)
                    for e in range(2):
                        r = slice(e * DH, (e + 1) * DH)
                        last = dve.tensor_scalar(k_bd[r, :, e, 0:WIN], k_bd[r, :, e, P:P + WIN], decay[r, :], None,
                                                 ALU.mult)
                    last.then_inc(halo, 1)
                if st.on(LG):
                    dve.wait_ge(y2t_ps, st.count(LG))
                    t0 = st.tile(LG) * P
                    lo, hi = stream[0:HALF, bass.ds(t0, P)], stream[HALF:P, bass.ds(t0 + 1, P)]
                    bias = bass.ds(st.layer(LG), 1)
                    dve.scalar_tensor_tensor(lo, H[1][0:HALF, 0:P], b2_col[0:HALF, bias], lo, ALU.add, ALU.add)
                    dve.scalar_tensor_tensor(hi, H[1][HALF:P, 0:P], b2_col[HALF:P, bias], hi, ALU.add, ALU.add)\
                       .then_inc(stream_ready, 1)
                if st.on(LX):
                    settled(dve, ln_stats)
                    wait(dve, proj_v, st.count(LX, 2))
                    settled(dve, ln_stats)
                    dve.wait_ge(stream_ready, stream_count(st, LX))
                    dve.tensor_copy(xs[st.par(LX)], stream[:, bass.ds(st.tile(LX) * P, P)]).then_inc(xs_ready, 1)
                if st.on(LP):
                    normalise(0, add_q, rn_q, rot_q)
                if st.on(LS):
                    dve.wait_ge(exp_done, st.count(LS))
                    dve.tensor_reduce(ssum, prob.rearrange("p (h k) -> p h k", k=SLOTS), AX, ALU.add)\
                       .then_inc(sum_done, 1)
                    dve.wait_ge(sum_done, st.count(LS))
                    dve.reciprocal(rsum[st.par(LS)], ssum).then_inc(rsum_done, 1)
                if st.on(LF):
                    dve.wait_ge(h_ps, st.count(LF))
                    b = st.par(LF)
                    off = (st.layer(LF) % 2) * 2 * HID
                    dve.tensor_tensor(hb[:, b, 0:HID], H[0][:, 0:HID], b_1[:, bass.ds(off, HID)], ALU.add)
                    dve.tensor_tensor(hb[:, b, HID:2 * HID], H[1][:, 0:HID], b_1[:, bass.ds(off + HID, HID)], ALU.add)\
                       .then_inc(hb_done, 1)
                if st.on(LP):
                    normalise(1, add_k, rn_k, rot_k)

            def start(n, blk):
                layer_norm(n)
                if blk == 0:
                    dve.wait_ge(const_in, 16 * (7 + 6))
                    dve.tensor_copy(mask[:], mask_in)
                    dve.tensor_copy(ident_b[:], ident[:]).then_inc(cast_done, 1)
                zero_blocks(blk)
                dve.memset(hid, 0.0)
                for g in range(4):
                    dve.wait_ge(ln_ps, 4 * n + g + 1)
                    dve.tensor_copy(stream[0:HALF, g * 512:g * 512 + 512], T[g % 2][0:HALF, :])
                    dve.tensor_copy(stream[HALF:P, g * 512 + 1:g * 512 + 513], T[g % 2][HALF:P, :])\
                       .then_inc(ln_lo, 1)
                last = dve.memset(stream[HALF:P, 0:1], 0.0)
                last.then_inc(stream_ready, TILES)

            dve.wait_ge(x_in, 64)
            start(0, 0)
            steps(dve, 0, body)
            post(0)

            dve.memset(g_q, 0.0).then_inc(g_zero, 1)
            layer_norm(1)
            for g in range(4):
                if g == 0:
                    dve.wait_ge(g_win, 16 * 8)
                dve.wait_ge(g_v_ps, g + 1)
                dve.tensor_tensor(g_v[:, 4 * g:4 * g + 4, :], H[g % 2][:].rearrange("p (t d) -> p t d", d=D),
                                  g_bv.unsqueeze(1).to_broadcast([P, 4, D]), ALU.add).then_inc(g_v_sb, 1)
            dve.wait_ge(g_zps, 1)
            dve.tensor_scalar(g_dx, H[0][:, 0:TILES], g_b2, None, ALU.add).then_inc(g_zc, 1)
            dve.wait_ge(g_zc, 2)
            dve.tensor_scalar(g_dx, g_dx, 1.0, None, ALU.add).then_inc(g_zc, 1)
            dve.wait_ge(g_zc, 3)
            dve.reciprocal(g_dx, g_dx).then_inc(g_zc, 1)
            dve.wait_ge(g_zc, 4)
            for h in range(GH):
                last = dve.tensor_scalar(g_thr[:, :, h], g_dx, float(L), WINDOWS[h], ALU.mult, ALU.add)
            last.then_inc(g_thr_done, 1)
            dve.wait_ge(g_thr_done, 1)

            chunks_before = [0]

            def masked_scores(t, h):
                n = t * GH + h
                keys = L - t * P
                dve.tensor_scalar(g_mask[:, 0:keys], g_dist[:, 0:keys], g_thr[:, t, h:h + 1], -BIG,
                                  ALU.is_gt, ALU.mult).then_inc(g_msk, 1)
                dve.wait_ge(g_msk, n + 1)
                if n >= 2:
                    dve.wait_ge(g_tps, tgroups[n - 2][-1][0] + 1)
                nch = (keys + 511) // 512
                for c in range(nch):
                    w = min(512, keys - c * 512)
                    dve.wait_ge(g_sps, chunks_before[0] + c + 1)
                    bank = s_bank(chunks_before[0] + c)
                    last = dve.tensor_tensor_reduce(g_s[n % 2][:, c * 512:c * 512 + w], bank[:, 0:w],
                                                    g_mask[:, c * 512:c * 512 + w], 2.0 / float(L) ** 0.5, -3.0e38,
                                                    ALU.add, ALU.max, g_mx[:, n % 2, c:c + 1])
                    last.then_inc(g_smx, 1)
                chunks_before[0] += nch
                dve.wait_ge(g_smx, chunks_before[0])
                dve.tensor_reduce(g_nm[:, n % 2:n % 2 + 1], g_mx[:, n % 2, 0:nch], AX, ALU.max, negate=True)\
                   .then_inc(g_nmx, 1)

            def evacuate(n, parity):
                for gidx, w in tgroups[n]:
                    if gidx % 2 == parity:
                        wait(dve, g_ops, n - 1)
                        dve.wait_ge(g_tps, gidx + 1)
                        c = gidx - tgroups[n][0][0]
                        dve.tensor_copy(g_pt[n % 2][:, c * 512:c * 512 + w], T[gidx % 2][:, 0:w]).then_inc(g_tev1, 1)

            def update(t):
                dve.wait_ge(g_ops2, t + 1)
                dve.wait_ge(g_exp, GH * (t + 1))
                b = t % 2
                dve.reciprocal(g_rs[:, GH * b:GH * b + GH], g_sum[:, GH * b:GH * b + GH]).then_inc(g_rsd, 1)
                dve.wait_ge(g_rsd, t + 1)
                for h in range(GH):
                    c = slice(h * GD, (h + 1) * GD)
                    last = dve.scalar_tensor_tensor(x_res[:, t, c], H[1][:, h * GD:(h + 1) * GD],
                                                    g_rs[:, GH * b + h:GH * b + h + 1], x_res[:, t, c],
                                                    ALU.mult, ALU.add)
                last.then_inc(g_upd, 1)

            UN = TILES * GH
            for n in range(UN + 3):
                if n < UN:
                    masked_scores(n // GH, n % GH)
                if 1 <= n <= UN:
                    evacuate(n - 1, 1)
                if n >= 6 and (n - 6) % GH == 0:
                    update((n - 6) // GH)
            dve.wait_ge(g_upd, TILES)

            start(2, 1)
            steps(dve, 1, body)
            post(1)

        @block.scalar
        def _(act):
            def body(st):
                if st.on(LO):
                    for n in range(2):
                        act.wait_ge(pt_ps, 2 * st.count(LO) - 1 + n)
                        act.activation(prob_t[:, n * 512:(n + 1) * 512], T[n][:], ACT.Copy).then_inc(pt_sb, 1)
                if st.on(LP):
                    act.wait_ge(proj_q, st.count(LP))
                    wait(act, add_q, st.count(LP, 1))
                    act.activation(raw[0], A[:], ACT.Copy).then_inc(raw_q, 1)
                if st.on(LS):
                    for n in range(2):
                        act.wait_ge(qt_ps, 2 * st.count(LS) - 1 + n)
                        act.activation(q_t[:, n * 512:(n + 1) * 512], T[n][:], ACT.Copy).then_inc(qt_sb, 1)
                if st.on(LP):
                    wait(act, red_k, st.count(LP, 1))
                    act.activation(square, A[:], ACT.Square).then_inc(sq_q, 1)
                if st.on(LS):
                    wait(act, halo, st.count(LS, 1))
                    for n in range(2):
                        act.wait_ge(kt_ps, 2 * st.count(LS) - 1 + n)
                        for e in range(2):
                            r = slice(e * DH, (e + 1) * DH)
                            last = act.activation(k_bd[r, 4 * n:4 * n + 4, e, WIN:WIN + P],
                                                  T[n][r, :].rearrange("p (c t) -> p c t", c=4), ACT.Copy)
                        last.then_inc(kt_sb, 1)
                if st.on(LG) and st.j == 0:
                    act.wait_ge(hb_done, st.base + st.s - LG + 2)
                    wait(act, hid_done, st.base // 2 + (st.s - LG) // 2)
                    act.activation(gelu, hb[:, :, HID:2 * HID], ACT.Gelu).then_inc(gelu_done, 1)
                if st.on(LP):
                    act.wait_ge(proj_k, st.count(LP))
                    wait(act, add_k, st.count(LP, 1))
                    act.activation(raw[1], A[:], ACT.Copy).then_inc(raw_k, 1)
                    act.wait_ge(red_q, st.count(LP))
                    act.activation(square, A[:], ACT.Square).then_inc(sq_k, 1)
                if st.on(LF):
                    act.wait_ge(xnt_ps, st.count(LF))
                    lay = bass.ds(st.layer(LF), 1)
                    act.activation(xn_t, H[0][:, 0:P], ACT.Identity, bias=ln_b[:, lay], scale=ln_g[:, lay])\
                       .then_inc(xnt_sb, 1)
                if st.on(LG):
                    act.wait_ge(ht_ps, st.count(LG))
                    act.activation(hid_t, H[1][:, 0:HCH * P], ACT.Copy).then_inc(ht_sb, 1)
                if st.on(LO):
                    for n in range(2):
                        act.wait_ge(ot_ps, 2 * st.count(LO) - 1 + n)
                        act.activation(o_t[:, n * 512:(n + 1) * 512], T[n][:], ACT.Copy).then_inc(ot_sb, 1)
                if st.on(LG):
                    act.wait_ge(y2_ps, st.count(LG))
                    act.activation(y2, H[1][:, 0:D], ACT.Copy).then_inc(y2_sb, 1)
                if st.on(LS):
                    act.wait_ge(sub_done, st.count(LS))
                    act.activation(prob, prob, ACT.Exp).then_inc(exp_done, 1)
                if st.on(LP):
                    act.wait_ge(proj_v, st.count(LP))
                    wait(act, v_dma[st.par(LP)], 8 * 16 * st.count2(LP, 2))
                    wait(act, v_halo[st.par(LP)], 2 * 16 * st.count2(LP, 2))
                    act.activation(v_tok[st.par(LP)].rearrange("p (e c d) -> p c e d", e=2, d=DH),
                                   A[:].rearrange("p (c e d) -> p c e d", e=2, d=DH), ACT.Copy).then_inc(v_ready, 1)
                if st.on(LO):
                    act.wait_ge(y1_ps, st.count(LO))
                    wait(act, y1t_ps, st.count(LO, 1))
                    act.activation(y1, T[0][:, 0:D], ACT.Copy).then_inc(y1_sb, 1)

            steps(act, 0, body)

            for g in range(4):
                act.wait_ge(ln_ps, 4 + g + 1)
                act.activation(g_xt[:, g * 512:(g + 1) * 512], T[g % 2][:], ACT.Copy).then_inc(ln_lo, 1)
            for g in range(4):
                bank = A[:, (g % 2) * 512:(g % 2) * 512 + 512]
                act.wait_ge(g_qin, g + 1)
                act.activation(g_in[:, g * 512:(g + 1) * 512], bank, ACT.Copy).then_inc(g_qin_sb, 1)
                act.activation(g_relu[:, g * 512:(g + 1) * 512], bank, ACT.Relu).then_inc(g_relu_sb, 1)
            act.wait_ge(g_zero, 1)
            act.wait_ge(g_win, 16 * 8)
            for g in range(4):
                for c in range(2):
                    bank = S[:, c * 512:c * 512 + 512]
                    act.wait_ge(g_qk_ps, 2 * g + c + 1)
                    if c == 0:
                        for h in range(GH):
                            r = slice(h * GD, (h + 1) * GD)
                            last = act.activation(g_q[r, h, g * 512:(g + 1) * 512], bank[r, :], ACT.Identity,
                                                  bias=g_bqk[r, 0:1])
                    else:
                        last = act.activation(g_k[:, g * 512:(g + 1) * 512], bank, ACT.Identity, bias=g_bqk[:, 1:2])
                    last.then_inc(g_qk_sb, 1)
            for g in range(4):
                act.wait_ge(g_hps, g + 1)
                act.activation(g_h[0:LEARNED, g * 512:(g + 1) * 512],
                               A[0:LEARNED, (g % 2) * 512:(g % 2) * 512 + 512], ACT.Copy).then_inc(g_hsb, 1)
            act.wait_ge(g_zc, 1)
            act.activation(g_dx, g_dx, ACT.Exp, scale=-1.0).then_inc(g_zc, 1)

            UN = TILES * GH
            for n in range(UN + 3):
                if n < UN:
                    t, h = n // GH, n % GH
                    act.wait_ge(g_nmx, n + 1)
                    if t >= 2:
                        act.wait_ge(g_rsd, t - 1)
                    act.activation(g_s[n % 2][:, 0:L - t * P], g_s[n % 2][:, 0:L - t * P], ACT.Exp,
                                   bias=g_nm[:, n % 2:n % 2 + 1],
                                   accum_out=g_sum[:, GH * (t % 2) + h:GH * (t % 2) + h + 1]).then_inc(g_exp, 1)
                if 1 <= n <= UN:
                    for gidx, w in tgroups[n - 1]:
                        if gidx % 2 == 0:
                            wait(act, g_ops, n - 2)
                            act.wait_ge(g_tps, gidx + 1)
                            c = gidx - tgroups[n - 1][0][0]
                            act.activation(g_pt[(n - 1) % 2][:, c * 512:c * 512 + w], T[0][:, 0:w], ACT.Copy)\
                               .then_inc(g_tev, 1)
                if n >= 6 and (n - 6) % GH == 0:
                    t = (n - 6) // GH
                    act.wait_ge(g_ops, GH * (t + 1))
                    wait(act, g_ops2, t)
                    act.activation(g_ot, H[0][:, 0:P], ACT.Copy).then_inc(g_otsb, 1)

            steps(act, 1, body)

        @block.tensor
        def _(pe):
            def ln_transposes(n):
                pe.wait_ge(ln_norm, n + 1)
                if n == 0:
                    pe.wait_ge(const_in, 16 * (7 + 6))
                for g in range(4):
                    if g >= 2 or n:
                        wait(pe, ln_lo, 4 * n + g - 1)
                    for k in range(4):
                        t = 4 * g + k
                        last = pe.transpose(T[g % 2][:, k * P:(k + 1) * P], ln_out(n)[:, t * D:(t + 1) * D], ident[:])
                    last.then_inc(ln_ps, 1)

            def post(n):
                wait(pe, stream_ready, (n + 1) * STREAM0)
                for g in range(4):
                    if g >= 2 or n:
                        wait(pe, post_add, 4 * n + g - 1)
                    for k in range(4):
                        t = 4 * g + k
                        lo, hi = post_banks(g)
                        pe.transpose(lo[:, k * HALF:(k + 1) * HALF], stream[0:HALF, t * P:(t + 1) * P],
                                     ident[0:HALF, 0:HALF])
                        last = pe.transpose(hi[:, k * HALF:(k + 1) * HALF],
                                            stream[HALF:P, t * P + 1:(t + 1) * P + 1], ident[HALF:P, HALF:P])
                    last.then_inc(post_ps, 1)

            def body(st):
                def weights(lag, per):
                    return (st.layer(lag) % 2) * per
                def transposes(dst, src, s, n):
                    for k in range(4):
                        c = 4 * n + k
                        last = pe.transpose(dst[:, k * P:(k + 1) * P], src[:, c * P:(c + 1) * P], ident[:])
                    last.then_inc(s, 1)
                def project(part, sem_out, free, value):
                    wait(pe, free, value)
                    for n in range(2):
                        off = weights(LP, 3 * INNER) + part * INNER + n * 512
                        last = pe.matmul(A[:, n * 512:(n + 1) * 512], xs[st.par(LP)], w_qkv[:, bass.ds(off, 512)],
                                         start=True, stop=True)
                    last.then_inc(sem_out, 1)
                if st.on(LO):
                    pe.wait_ge(exp_done, st.count(LO))
                    wait(pe, kt_sb, 2 * st.count(LO))
                    wait(pe, y1_sb, st.count(LO, 1))
                    transposes(T[0], prob, pt_ps, 0)
                    transposes(T[1], prob, pt_ps, 1)
                if st.on(LP):
                    pe.wait_ge(xs_ready, st.count(LP))
                    pe.wait_ge(w_in, 16 * W_DMAS * (st.base // UNITS * DEPTH + st.layer(LP) + 1))
                    project(0, proj_q, v_ready, st.count(LP, 1))
                if st.on(LS):
                    pe.wait_ge(rot_q, st.count(LS))
                    for n in range(2):
                        if st.on(LO):
                            pe.wait_ge(pt_sb, 2 * st.count(LO) - 1 + n)
                        else:
                            wait(pe, kt_sb, 2 * st.count(LS, 1))
                        transposes(T[n], rot[0], qt_ps, n)
                if st.on(LF):
                    pe.wait_ge(y1_sb, st.count(LF))
                    wait(pe, hb_done, st.count(LF, 1))
                    pe.transpose(H[0][:, 0:P], y1, ident[:]).then_inc(y1t_ps, 1)
                if st.on(LO):
                    pe.wait_ge(v_dma[st.par(LO)], 8 * 16 * st.count2(LO))
                    wait(pe, v_halo[st.par(LO + 1)], 2 * 16 * st.count2(LO, 1))
                    for n in range(2):
                        pe.wait_ge(pt_sb, 2 * st.count(LO) - 1 + n)
                        for c in range(4 * n, 4 * n + 4):
                            for w in range(WINS):
                                v = v_win[st.par(LO)][w].rearrange("p (e c d) -> p c e d", e=2, d=DH)
                                last = pe.matmul(S[w * WIN:(w + 1) * WIN, c * P:(c + 1) * P],
                                                 prob_t[:, c * P + w * WIN:c * P + (w + 1) * WIN], v[:, c],
                                                 start=True, stop=True)
                    last.then_inc(av_ps, 1)
                if st.on(LS):
                    pe.wait_ge(rot_k, st.count(LS))
                    for n in range(2):
                        pe.wait_ge(qt_sb, 2 * st.count(LS) - 1 + n)
                        transposes(T[n], rot[1], kt_ps, n)
                if st.on(LF):
                    pe.wait_ge(xs2_ready, st.count(LF))
                    pe.transpose(H[0][:, 0:P], xs2, ident[:]).then_inc(f1_ps, 1)
                if st.on(LP):
                    project(1, proj_k, sq_q, st.count(LP))
                if st.on(LS):
                    if st.on(LO):
                        pe.wait_ge(o_ready, st.count(LO))
                    for n in range(2):
                        pe.matmul(S[:, n * 512:(n + 1) * 512], ident_b[:],
                                  mask[:, bass.ds(st.tile(LS), 1), :].to_broadcast([P, 8, SLOTS]),
                                  start=True, stop=True)
                    for n in range(2):
                        pe.wait_ge(kt_sb, 2 * st.count(LS) - 1 + n)
                        for c in range(4 * n, 4 * n + 4):
                            for w in range(WINS):
                                last = pe.matmul(S[w * WIN:(w + 1) * WIN, c * P:(c + 1) * P],
                                                 q_t[:, c * P + w * WIN:c * P + (w + 1) * WIN],
                                                 k_bd[:, c, :, w * WIN:w * WIN + SLOTS],
                                                 start=False, stop=True, skip_group_check=True)
                    last.then_inc(scores_ps, 1)
                if st.on(LF):
                    pe.wait_ge(xn_ready, st.count(LF))
                    pe.transpose(H[0][:, 0:P], xn, ident[:]).then_inc(xnt_ps, 1)
                if st.on(LG):
                    if st.j == 0:
                        pe.wait_ge(hid_done, st.base // 2 + (st.s - LG) // 2 + 1)
                    if st.on(LF):
                        wait(pe, hb_done, st.count(LF, 1))
                    else:
                        wait(pe, hb_done, st.base + UNITS)
                        wait(pe, stream_ready, stream_count(st, LG) + TILES - 1)
                    for c in range(HCH):
                        last = pe.transpose(H[1][:, c * P:(c + 1) * P], hid[:, st.par(LG), c * P:(c + 1) * P], ident[:])
                    last.then_inc(ht_ps, 1)
                if st.on(LO):
                    pe.wait_ge(o_ready, st.count(LO))
                    for n in range(2):
                        if st.on(LS):
                            pe.wait_ge(kt_sb, 2 * st.count(LS) - 1 + n)
                        else:
                            pe.wait_ge(pt_sb, 2 * st.count(LO) - 1 + n)
                        transposes(T[n], o_tok, ot_ps, n)
                if st.on(LG):
                    pe.wait_ge(ht_sb, st.count(LG))
                    for c in range(HCH):
                        k = min(P, HID - c * P)
                        off = weights(LG, HCH * D) + c * D
                        last = pe.matmul(H[1][:, 0:D], hid_t[0:k, c * P:(c + 1) * P], w_2[0:k, bass.ds(off, D)],
                                         start=(c == 0), stop=(c == HCH - 1))
                    last.then_inc(y2_ps, 1)
                if st.on(LP):
                    project(2, proj_v, sq_k, st.count(LP))
                if st.on(LG):
                    pe.wait_ge(y2_sb, st.count(LG))
                    pe.transpose(H[1][:, 0:P], y2, ident[:]).then_inc(y2t_ps, 1)
                if st.on(LO):
                    for n in range(2):
                        pe.wait_ge(ot_sb, 2 * st.count(LO) - 1 + n)
                        for c in range(4 * n, 4 * n + 4):
                            off = weights(LO, PAIRS * D) + c * D
                            last = pe.matmul(T[0][:, 0:D], o_t[:, c * P:(c + 1) * P],
                                             w_o[:, bass.ds(off, D)], start=(c == 0), stop=(c == PAIRS - 1))
                    last.then_inc(y1_ps, 1)
                if st.on(LF):
                    pe.wait_ge(xnt_sb, st.count(LF))
                    if st.on(LG):
                        pe.wait_ge(stream_ready, stream_count(st, LG) + TILES)
                    for n in range(2):
                        off = weights(LF, 2 * HID) + n * HID
                        last = pe.matmul(H[n][:, 0:HID], xn_t, w_1[:, bass.ds(off, HID)], start=True, stop=True)
                    last.then_inc(h_ps, 1)

            ln_transposes(0)
            pe.wait_ge(ln_lo, 4)
            pe.wait_ge(cast_done, 1)
            steps(pe, 0, body)
            post(0)

            pe.wait_ge(post_add, 4)
            ln_transposes(1)
            pe.wait_ge(g_win, 16 * 8)
            for g in range(4):
                pe.wait_ge(ln_lo, 4 + g + 1)
                if g >= 2:
                    pe.wait_ge(g_relu_sb, g - 1)
                pe.matmul(A[:, (g % 2) * 512:(g % 2) * 512 + 512], g_w[:, 0:D], g_xt[:, g * 512:(g + 1) * 512],
                          start=True, stop=True).then_inc(g_qin, 1)
            for g in range(4):
                pe.wait_ge(g_qin_sb, g + 1)
                for c in range(2):
                    wait(pe, g_qk_sb, 2 * g + c - 1)
                    pe.matmul(S[:, c * 512:c * 512 + 512], g_w[:, D + c * D:2 * D + c * D],
                              g_in[:, g * 512:(g + 1) * 512], start=True, stop=True).then_inc(g_qk_ps, 1)
            for g in range(4):
                wait(pe, g_v_sb, g - 1)
                for k in range(4):
                    t = 4 * g + k
                    last = pe.matmul(H[g % 2][:, k * D:(k + 1) * D], g_in[:, t * P:(t + 1) * P],
                                     g_w[:, 3 * D:4 * D], start=True, stop=True)
                last.then_inc(g_v_ps, 1)
            for g in range(4):
                pe.wait_ge(g_relu_sb, 4)
                wait(pe, g_hsb, g - 1)
                pe.matmul(A[0:LEARNED, (g % 2) * 512:(g % 2) * 512 + 512], g_w[:, 4 * D:4 * D + LEARNED],
                          g_relu[:, g * 512:(g + 1) * 512], start=True, stop=True).then_inc(g_hps, 1)
            pe.wait_ge(g_hsb, 4)
            pe.wait_ge(g_v_sb, 4)
            for t in range(TILES):
                last = pe.matmul(H[0][:, t:t + 1], g_h[0:LEARNED, t * P:(t + 1) * P],
                                 g_w[0:LEARNED, 4 * D + LEARNED:4 * D + LEARNED + 1], start=True, stop=True)
            last.then_inc(g_zps, 1)
            pe.wait_ge(g_qk_sb, 8)

            UN = TILES * GH
            done = [0]
            tdone = [0]
            for n in range(UN + 3):
                if n < UN:
                    t, h = n // GH, n % GH
                    keys = L - t * P
                    for c in range((keys + 511) // 512):
                        w = min(512, keys - c * 512)
                        if done[0] >= 4:
                            pe.wait_ge(g_smx, done[0] - 3)
                        pe.matmul(s_bank(done[0])[:, 0:w], g_q[:, h, t * P:(t + 1) * P],
                                  g_k[:, t * P + c * 512:t * P + c * 512 + w], start=True, stop=True)\
                          .then_inc(g_sps, 1)
                        done[0] += 1
                if 1 <= n <= UN:
                    m = n - 1
                    pe.wait_ge(g_exp, m + 1)
                    for gidx, w in tgroups[m]:
                        if gidx >= 2:
                            pe.wait_ge(g_tev if gidx % 2 == 0 else g_tev1, gidx // 2)
                        c = gidx - tgroups[m][0][0]
                        for k in range(w // P):
                            last = pe.transpose(T[gidx % 2][:, k * P:(k + 1) * P],
                                                g_s[m % 2][:, c * 512 + k * P:c * 512 + (k + 1) * P], ident[:])
                        last.then_inc(g_tps, 1)
                if 2 <= n <= UN + 1:
                    m = n - 2
                    t, h = m // GH, m % GH
                    nt = TILES - t
                    last_g = tgroups[m][-1][0]
                    pe.wait_ge(g_tev, last_g // 2 + 1 if last_g % 2 == 0 else (last_g + 1) // 2)
                    wait(pe, g_tev1, (last_g + 1) // 2)
                    if h == 0:
                        if t == 0:
                            pe.wait_ge(g_zc, 1)
                        else:
                            pe.wait_ge(g_otsb, t)
                    for k in range(nt):
                        last = pe.matmul(H[0][h * GD:(h + 1) * GD, 0:P], g_v[:, t + k, h * GD:(h + 1) * GD],
                                         g_pt[m % 2][:, k * P:(k + 1) * P], start=(k == 0), stop=(k == nt - 1))
                    last.then_inc(g_ops, 1)
                if n >= 6 and (n - 6) % GH == 0:
                    t = (n - 6) // GH
                    pe.wait_ge(g_otsb, t + 1)
                    wait(pe, g_upd, t)
                    pe.transpose(H[1][:, 0:P], g_ot, ident[:]).then_inc(g_ops2, 1)
            ln_transposes(2)
            pe.wait_ge(ln_lo, 12)
            steps(pe, 1, body)
            post(1)


def constants():
    import numpy as np

    half = np.arange(0, DH, 2, dtype=np.float32)
    inv_freq = (1.0 / np.power(np.float32(10000.0), half / np.float32(DH))).astype(np.float32)
    t = np.arange(L, dtype=np.float32)
    angle = (t[:, None] * inv_freq[None, :]).astype(np.float64)
    base = (half.astype(np.float64) + 0.4 * DH) / (1.4 * DH)
    power = (np.arange(L) % P - P // 2) / (WIN // 2)
    scale = base[None, :] ** power[:, None]
    cos, sin = np.cos(angle), np.sin(angle)
    rope = np.concatenate([cos * scale, cos * scale, -sin * scale, sin * scale], 1) * QK_SCALE
    rope_k = np.concatenate([cos / scale, cos / scale, -sin / scale, sin / scale], 1)
    rope = np.concatenate([rope, rope_k], 1).astype(np.float32).reshape(TILES, P, 4 * DH).transpose(1, 0, 2)
    decay = np.tile(base ** (P // (WIN // 2)), 4).astype(np.float32)[:, None]
    a, b = np.arange(P)[:, None] % WIN, np.arange(SLOTS)[None, :]
    seen = np.broadcast_to(((b >= a) & (b <= a + WIN))[:, None, :], (P, TILES, SLOTS)).copy()
    seen[0:WIN, 0, 0:WIN] = False
    mask = np.where(seen, 0.0, NEG).astype(np.float32)
    dist = (np.arange(L)[None, :] - np.arange(P)[:, None]).astype(np.float32)
    dist[dist < 0] = 1e9
    eye = np.eye(P, dtype=np.float32)
    return {"c_rope": np.ascontiguousarray(rope), "c_decay": decay, "c_mask": mask, "c_ident": eye, "c_dist": dist}


def kernel(**inputs):
    import numpy as np
    import concourse.bacc as bacc
    from concourse.bass_utils import run_bass_kernel_spmd

    a = {k: np.asarray(v) for k, v in inputs.items()}
    w2 = a["L0_ffn_W2"]
    w2 = np.concatenate([w2, np.zeros((DEPTH, HCH * P - HID, D), w2.dtype)], 1)
    b = a["L0_attn_bqkv"]
    arrays = {
        "x": a["L0_attn_x"], "fWqkv": a["L0_ffn_Wqkv"], "fqs": a["L0_ffn_q_scale"], "fks": a["L0_ffn_k_scale"],
        "fWo": a["L0_ffn_Wo"], "fg": a["L0_ffn_ln_g"].T, "fb": a["L0_ffn_ln_b"].T, "fW1": a["L0_ffn_W1"],
        "fb1": a["L0_ffn_b1"], "fW2": w2.reshape(DEPTH, HCH, P, D).transpose(0, 2, 1, 3), "fb2": a["L0_ffn_b2"].T,
        "aWqT": a["L0_attn_Wq"].T, "aWqkvT": a["L0_attn_Wqkv"].T, "abqkT": b[0:2 * D].reshape(2, D).T,
        "abv": b[2 * D:3 * D], "aWopT": a["L0_attn_Wop"].T, "aW2T": a["L0_attn_W2"].T, "ab2": a["L0_attn_b2"],
    }
    arrays.update(constants())
    arrays = {k: np.ascontiguousarray(v) for k, v in arrays.items()}
    nc = bacc.Bacc("TRN2", target_bir_lowering=False, num_devices=1)
    args = {k: nc.dram_tensor(k, v.shape, mybir.dt.from_np(v.dtype), kind="ExternalInput").ap()
            for k, v in arrays.items()}
    out = nc.dram_tensor("out", (1, L, D), F32, kind="ExternalOutput").ap()
    build(nc, out=out, **args)
    r = run_bass_kernel_spmd(nc, [arrays], core_ids=[0])
    return r.results[0]["out"]
```

```python
from contextlib import ExitStack

import concourse.bass as bass
from concourse import mybir

F32 = mybir.dt.float32
BF16 = mybir.dt.bfloat16
ALU = mybir.AluOpType
ACT = mybir.ActivationFunctionType
AX = mybir.AxisListType.X

P = 128
L = 2048
D = 128
HALF = D // 2
TILES = L // P
DEPTH = 6
HEADS = 16
DH = 64
PAIRS = HEADS // 2
INNER = HEADS * DH
WIN = 32
WINS = P // WIN
SLOTS = 2 * WIN
HID = int(D * 4 * 2 / 3)
HCH = (HID + P - 1) // P
UNITS = DEPTH * TILES
EPS = 1e-5
QK_SCALE = 8.0
NEG = -1e30

LX, LP, LS, LO, LF, LG = 0, 1, 2, 3, 4, 6
ITERS = (UNITS + LG) // 2
FIRST, LAST = LG // 2 + 1, UNITS // 2

GH = 4
GD = D // GH
LEARNED = 32
WINDOWS = (32.0, 64.0, 128.0, 256.0)
BIG = 1e18


class Step:

    def __init__(self, i, j, block, fixed):
        self.i, self.s, self.j, self.base, self.fixed = i, i * 2 + j, j, block * UNITS, fixed

    def on(self, lag):
        return not self.fixed or 0 <= self.s - lag < UNITS

    def unit(self, lag):
        return self.s - lag

    def par(self, lag):
        return (self.j - lag) % 2

    def tile(self, lag):
        return (self.s - lag) % TILES

    def layer(self, lag):
        return (self.s - lag) // TILES

    def count(self, lag, back=0):
        return self.base + (self.s - lag - back + 1)

    def count2(self, lag, back=0):
        return self.i + (self.base // 2 + (self.j - lag - back) // 2 + 1)


def wait(eng, sem, value):
    if isinstance(value, int) and value <= 0:
        return
    eng.wait_ge(sem, value)


def settled(eng, sem):
    eng.wait_ge(sem, 1)


def steps(eng, block, body):
    def both(i, fixed):
        for j in range(2):
            body(Step(i, j, block, fixed))
    for i in range(FIRST):
        both(i, True)
    with eng.Fori(FIRST, LAST) as i:
        both(i, False)
    for i in range(LAST, ITERS):
        both(i, True)


def build(nc, x, fWqkv, fqs, fks, fWo, fg, fb, fW1, fb1, fW2, fb2,
          aWqT, aWqkvT, abqkT, abv, aWopT, aW2T, ab2,
          c_rope, c_decay, c_mask, c_ident, c_dist, out):
    ctx = ExitStack()
    with ctx:
        def sb(name, shape, dt=F32):
            return ctx.enter_context(nc.sbuf_tensor(name, shape, dt))

        def sem(name):
            return ctx.enter_context(nc.semaphore(name))

        x_res = sb("x_res", [P, TILES, D])
        stream = sb("stream", [P, L + 2])
        rope = sb("rope", [P, TILES, 4 * DH])
        qk_gain = sb("qk_gain", [P, DEPTH, 4 * DH])
        mask = sb("mask", [P, TILES, SLOTS], BF16)
        ident = sb("ident", [P, P])
        ident_b = sb("ident_b", [P, P], BF16)
        decay = sb("decay", [P, 1])
        half_pow = sb("half_pow", [P, TILES])
        ln_g = sb("ln_g", [P, DEPTH])
        ln_b = sb("ln_b", [P, DEPTH])
        b2_col = sb("b2_col", [P, DEPTH])
        w_qkv = sb("w_qkv", [P, 2 * 3 * INNER])
        w_o = sb("w_o", [P, 2 * PAIRS * D])
        w_1 = sb("w_1", [P, 2 * 2 * HID])
        w_2 = sb("w_2", [P, 2 * HCH * D])
        b_1 = sb("b_1", [P, 2 * 2 * HID])
        stats = sb("stats", [P, TILES, 6])
        mv = sb("mv", [P, TILES, 2])
        rstd = sb("rstd", [P, TILES])
        ARENA = 28832
        arena = sb("arena", [P, ARENA])

        used = [0]

        def carve(n):
            a = arena[:, used[0]:used[0] + n]
            used[0] += n
            assert used[0] <= ARENA, used[0]
            return a

        v_win = [[carve(2 * PAIRS * DH) for _ in range(WINS)] for _ in range(2)]
        k_bd = carve(PAIRS * 2 * (WIN + P)).rearrange("p (c e t) -> p c e t", c=PAIRS, e=2)
        zeroed = used[0]
        xs = [carve(P) for _ in range(2)]
        xs2 = carve(P)
        table = [carve(4 * DH) for _ in range(2)]
        raw = [carve(INNER) for _ in range(2)]
        ln_scratch = arena[:, used[0] - 2 * INNER:used[0]]
        square = carve(INNER)
        swapped = carve(INNER)
        rot = [carve(INNER) for _ in range(2)]
        q_t = carve(INNER)
        prob = carve(HEADS * SLOTS)
        mask_in = prob.rearrange("p (t k) -> p t k", k=SLOTS)
        prob_t = carve(INNER)
        v_tok = [carve(INNER) for _ in range(2)]
        o_tok = carve(INNER)
        o_t = carve(INNER)
        y1 = carve(D)
        y2 = carve(D)
        xn = carve(D)
        xn_t = carve(D)
        hb = carve(2 * 2 * HID).rearrange("p (b n) -> p b n", b=2)
        gelu = carve(2 * HID).rearrange("p (b n) -> p b n", b=2)
        hid = carve(2 * HCH * P).rearrange("p (b n) -> p b n", b=2)
        hid_t = carve(HCH * P)
        ss = carve(2 * HEADS)
        rn = carve(2 * HEADS)
        smax = carve(HEADS)
        ssum = carve(HEADS)
        rsum = [carve(HEADS) for _ in range(2)]
        st1 = carve(6)
        mv1 = carve(2)
        rs1 = carve(1)
        ve1 = carve(1)

        used[0] = 0
        g_q = carve(GH * L).rearrange("p (h t) -> p h t", h=GH)
        g_k = carve(L)
        g_v = carve(L).rearrange("p (t d) -> p t d", d=D)
        g_dist = carve(L)
        g_s = [carve(L) for _ in range(2)]
        g_mask = carve(L)
        g_pt = [carve(L) for _ in range(2)]
        g_in = carve(L)
        g_relu = g_pt[0]
        g_xt = g_s[0]
        g_h = g_s[1]
        g_w = carve(D + 3 * D + LEARNED + 1)
        g_bqk = carve(2)
        g_bv = carve(D)
        g_b2 = carve(1)
        g_thr = carve(TILES * GH).rearrange("p (t h) -> p t h", h=GH)
        g_dx = carve(TILES)
        g_mx = carve(2 * 4).rearrange("p (b c) -> p b c", b=2)
        g_nm = carve(2)
        g_sum = carve(GH * 2)
        g_rs = carve(GH * 2)
        g_ot = carve(P)

        tgroups, total = [], 0
        for n in range(TILES * GH):
            keys = L - n // GH * P
            tgroups.append([(total + c, min(512, keys - c * 512)) for c in range((keys + 511) // 512)])
            total += len(tgroups[-1])

        def ln_out(n):
            return g_mask if n == 1 else ln_scratch

        A = ctx.enter_context(nc.psum_tensor("ps_a", [P, 1024], F32))
        T = [ctx.enter_context(nc.psum_tensor(f"ps_t{n}", [P, 512], F32)) for n in range(2)]
        S = ctx.enter_context(nc.psum_tensor("ps_s", [P, 1024], F32))
        H = [ctx.enter_context(nc.psum_tensor(f"ps_h{n}", [P, 512], F32)) for n in range(2)]

        def s_bank(k):
            return (A, S)[k // 2 % 2][:, k % 2 * 512:k % 2 * 512 + 512]

        def post_banks(g):
            return (T[0], T[1]) if g % 2 == 0 else (A[:, 0:512], A[:, 512:1024])

        (const_in, x_in, w_in, g_win, zero_done, misc_done, cast_done, g_zero, out_done) = map(
            sem, "const_in x_in w_in g_win zero_done misc_done cast_done g_zero out_done".split())
        (ln_stats, ln_mv, ln_rstd, ln_norm, ln_ps, ln_lo) = map(
            sem, "ln_stats ln_mv ln_rstd ln_norm ln_ps ln_lo".split())
        post_ps, post_add = map(sem, "post_ps post_add".split())
        stream_ready, xs_ready, table_ready = map(sem, "stream_ready xs_ready table_ready".split())
        (proj_q, proj_k, proj_v, raw_q, raw_k, sq_q, sq_k, v_ready) = map(
            sem, "proj_q proj_k proj_v raw_q raw_k sq_q sq_k v_ready".split())
        v_dma0, v_dma1, v_halo0, v_halo1 = map(sem, "v_dma0 v_dma1 v_halo0 v_halo1".split())
        (t1_q, t1_k, red_q, red_k, guard_q, guard_k, rn_q, rn_k) = map(
            sem, "t1_q t1_k red_q red_k guard_q guard_k rn_q rn_k".split())
        sw_q, sw_k, add_q, add_k, rot_q, rot_k = map(sem, "sw_q sw_k add_q add_k rot_q rot_k".split())
        qt_ps, qt_sb, kt_ps, kt_sb, halo = map(sem, "qt_ps qt_sb kt_ps kt_sb halo".split())
        (scores_ps, max_done, sub_done, exp_done, sum_done, rsum_done) = map(
            sem, "scores_ps max_done sub_done exp_done sum_done rsum_done".split())
        (pt_ps, pt_sb, av_ps, o_ready, ot_ps, ot_sb, y1_ps, y1_sb, y1t_ps) = map(
            sem, "pt_ps pt_sb av_ps o_ready ot_ps ot_sb y1_ps y1_sb y1t_ps".split())
        (attn_res, xs2_ready, f1_ps, bn_done, mv_done, ve_done, rs_done, xn_ready, xnt_ps, xnt_sb) = map(
            sem, "attn_res xs2_ready f1_ps bn_done mv_done ve_done rs_done xn_ready xnt_ps xnt_sb".split())
        (h_ps, hb_done, gelu_done, hid_done, ht_ps, ht_sb, y2_ps, y2_sb, y2t_ps) = map(
            sem, "h_ps hb_done gelu_done hid_done ht_ps ht_sb y2_ps y2_sb y2t_ps".split())
        g_qin, g_qin_sb, g_relu_sb, g_qk_ps, g_q_sb, g_k_sb = map(
            sem, "g_qin g_qin_sb g_relu_sb g_qk_ps g_q_sb g_k_sb".split())
        g_v_ps, g_v_sb, g_hps, g_hsb, g_zps, g_zc, g_thr_done = map(
            sem, "g_v_ps g_v_sb g_hps g_hsb g_zps g_zc g_thr_done".split())
        g_sps, g_msk, g_smx, g_nmx, g_exp = map(sem, "g_sps g_msk g_smx g_nmx g_exp".split())
        g_tps, g_pt_act, g_pt_dve = map(sem, "g_tps g_pt_act g_pt_dve".split())
        g_ops, g_otsb, g_ops2, g_rsd, g_upd = map(sem, "g_ops g_otsb g_ops2 g_rsd g_upd".split())
        v_dma, v_halo = (v_dma0, v_dma1), (v_halo0, v_halo1)
        CONST_DMAS = 7 + 6
        W_DMAS = 5
        G_DMAS = 8
        V_DMAS = 2 * WINS
        HALO_DMAS = 2
        STREAM0 = TILES + UNITS

        def stream_count(step, lag):
            return step.base // UNITS * STREAM0 + step.s - lag + 1

        block = ctx.enter_context(nc.Block())

        @block.sync
        def _(sp):
            for t0 in range(0, TILES, 4):
                sp.dma_start(x_res[:, t0:t0 + 4, :],
                             x[0].rearrange("(t p) d -> p t d", p=P)[:, t0:t0 + 4, :]).then_inc(x_in, 16)
            for dst, src in ((ident[:], c_ident), (rope[:], c_rope), (mask_in, c_mask),
                             (decay[:], c_decay), (ln_g[:], fg), (ln_b[:], fb), (b2_col[:], fb2)):
                sp.dma_start(dst, src).then_inc(const_in, 16)
            gain = qk_gain[:].rearrange("p l (a h d) -> p l a h d", a=4, h=2)
            for a, src in ((0, fqs), (2, fks)):
                row = src.rearrange("l (h d) -> l h d", h=2)
                sp.dma_start(qk_gain[:, :, a * DH:(a + 1) * DH], src.partition_broadcast(P)).then_inc(const_in, 16)
                for h in range(2):
                    sp.dma_start(gain[:, :, a + 1, h, :], row[:, 1 - h, :].partition_broadcast(P))\
                      .then_inc(const_in, 16)

            def load_layer(layer):
                par = layer % 2
                lay = bass.ds(layer, 1)
                sp.dma_start(w_qkv[:, bass.ds(par * 3 * INNER, 3 * INNER)],
                             fWqkv[lay].rearrange("a p n -> p (a n)")).then_inc(w_in, 16)
                sp.dma_start(w_o[:, bass.ds(par * PAIRS * D, PAIRS * D)].rearrange("p (c n) -> p c n", c=PAIRS),
                             fWo[lay].rearrange("a (c p) n -> p (a c) n", p=P)).then_inc(w_in, 16)
                sp.dma_start(w_1[:, bass.ds(par * 2 * HID, 2 * HID)],
                             fW1[lay].rearrange("a p n -> p (a n)")).then_inc(w_in, 16)
                sp.dma_start(w_2[:, bass.ds(par * HCH * D, HCH * D)].rearrange("p (c n) -> p c n", c=HCH),
                             fW2[lay].rearrange("a p c n -> p (a c) n")).then_inc(w_in, 16)
                sp.dma_start(b_1[:, bass.ds(par * 2 * HID, 2 * HID)],
                             fb1[lay].rearrange("a n -> (a n)").partition_broadcast(P)).then_inc(w_in, 16)

            def spread_v(blk, unit, par):
                count = blk * UNITS + unit
                sp.wait_ge(v_ready, count + 1)
                for e in range(2):
                    cols = slice(e * PAIRS * DH, (e + 1) * PAIRS * DH)
                    row = e * SLOTS
                    sp.dma_start(v_win[par][0][row + WIN:row + SLOTS, cols],
                                 v_tok[par][0:WIN, cols]).then_inc(v_dma[par], 16)
                    for w in range(1, WINS):
                        sp.dma_start(v_win[par][w][row:row + SLOTS, cols],
                                     v_tok[par][(w - 1) * WIN:(w + 1) * WIN, cols]).then_inc(v_dma[par], 16)
                wait(sp, av_ps, count)
                for e in range(2):
                    cols = slice(e * PAIRS * DH, (e + 1) * PAIRS * DH)
                    sp.dma_start(v_win[1 - par][0][e * SLOTS:e * SLOTS + WIN, cols],
                                 v_tok[par][P - WIN:P, cols]).then_inc(v_halo[par], 16)

            def stack(blk):
                wait(sp, zero_done, 1 + blk)
                spread_v(blk, 0, 0)
                spread_v(blk, 1, 1)
                with sp.Fori(1, TILES // 4) as k:
                    for j in range(2):
                        spread_v(blk, k * 2 + j, j)
                load_layer(1)
                with sp.Fori(TILES // 4, TILES // 2) as k:
                    for j in range(2):
                        spread_v(blk, k * 2 + j, j)
                with sp.Fori(1, DEPTH - 1) as layer:
                    with sp.Fori(0, TILES // 4) as k:
                        for j in range(2):
                            spread_v(blk, layer * TILES + k * 2 + j, j)
                    load_layer(layer + 1)
                    with sp.Fori(TILES // 4, TILES // 2) as k:
                        for j in range(2):
                            spread_v(blk, layer * TILES + k * 2 + j, j)
                with sp.Fori((DEPTH - 1) * TILES // 2, DEPTH * TILES // 2) as k:
                    for j in range(2):
                        spread_v(blk, k * 2 + j, j)

            load_layer(0)
            stack(0)
            sp.wait_ge(post_add, 4)
            for dst, src in ((g_dist, c_dist), (g_w[:, 0:D], aWqT), (g_w[:, D:4 * D], aWqkvT),
                             (g_w[:, 4 * D:4 * D + LEARNED], aWopT),
                             (g_w[0:LEARNED, 4 * D + LEARNED:4 * D + LEARNED + 1], aW2T),
                             (g_bqk, abqkT), (g_bv, abv.partition_broadcast(P)), (g_b2, ab2.partition_broadcast(P))):
                sp.dma_start(dst, src).then_inc(g_win, 16)
            load_layer(0)
            stack(1)
            for g in range(4):
                sp.wait_ge(post_add, 4 + g + 1)
                sp.dma_start(out[0].rearrange("(t p) d -> p t d", p=P)[:, 4 * g:4 * g + 4, :],
                             x_res[:, 4 * g:4 * g + 4, :]).then_inc(out_done, 16)
            sp.wait_ge(out_done, 4 * 16)

        @block.gpsimd
        def _(pool):
            pool.memset(half_pow[:], -0.5).then_inc(misc_done, 1)

            def layer_norm_rstd(n):
                pool.wait_ge(ln_mv, n + 1)
                pool.tensor_scalar(rstd[:], mv[:, :, 1], EPS, None, ALU.add).then_inc(ln_rstd, 1)
                pool.wait_ge(ln_rstd, 2 * n + 1)
                pool.tensor_tensor(rstd[:], rstd[:], half_pow[:], ALU.pow).then_inc(ln_rstd, 1)

            def body(st):
                if st.on(LX):
                    if st.fixed and st.s == 0:
                        wait(pool, const_in, 16 * CONST_DMAS)
                    wait(pool, t1_k, st.count(LX, 2))
                    wait(pool, sw_k, st.count(LX, 2))
                    pool.tensor_tensor(table[st.par(LX)],
                                       rope[:, bass.ds(st.tile(LX), 1), :].rearrange("p a n -> p (a n)"),
                                       qk_gain[:, bass.ds(st.layer(LX), 1), :].rearrange("p a n -> p (a n)"),
                                       ALU.mult).then_inc(table_ready, 1)

                def swap_halves(n, raw_s, sw_s, used_s, used):
                    tab = table[st.par(LP)].rearrange("p (a h d) -> p a h d", a=4, h=2)[:, 2 * n + 1]
                    src = raw[n].rearrange("p (c h d) -> p c h d", h=2, d=DH // 2)
                    dst = swapped.rearrange("p (c h d) -> p c h d", h=2, d=DH // 2)
                    wait(pool, used_s, used)
                    pool.wait_ge(table_ready, st.count(LP))
                    pool.wait_ge(raw_s, st.count(LP))
                    for h in range(2):
                        last = pool.tensor_tensor(dst[:, :, h, :], src[:, :, 1 - h, :],
                                                  tab[:, h:h + 1, :].to_broadcast([P, HEADS, DH // 2]), ALU.mult)
                    last.then_inc(sw_s, 1)

                def add_swapped(n, sw_s, t1_s, add_s):
                    pool.wait_ge(sw_s, st.count(LP))
                    pool.wait_ge(t1_s, st.count(LP))
                    pool.tensor_tensor(rot[n], rot[n], swapped, ALU.add).then_inc(add_s, 1)

                def inverse_norm(n, guard_s, rn_s):
                    pool.wait_ge(guard_s, st.count(LP))
                    c = slice(n * HEADS, (n + 1) * HEADS)
                    pool.tensor_tensor(rn[:, c], ss[:, c], half_pow[:, 0:HEADS], ALU.pow).then_inc(rn_s, 1)

                if st.on(LP):
                    swap_halves(0, raw_q, sw_q, add_k, st.count(LP, 1))
                    add_swapped(0, sw_q, t1_q, add_q)
                if st.on(LF):
                    pool.wait_ge(ve_done, st.count(LF))
                    pool.tensor_tensor(rs1, ve1, half_pow[:, 0:1], ALU.pow).then_inc(rs_done, 1)
                if st.on(LP):
                    inverse_norm(0, guard_q, rn_q)
                    swap_halves(1, raw_k, sw_k, add_q, st.count(LP))
                    add_swapped(1, sw_k, t1_k, add_k)
                    inverse_norm(1, guard_k, rn_k)

            def zero_blocks():
                pool.memset(hid, 0.0)
                pool.memset(arena[:, 0:zeroed], 0.0).then_inc(zero_done, 1)

            zero_blocks()
            pool.wait_ge(misc_done, 1)
            layer_norm_rstd(0)
            steps(pool, 0, body)
            pool.wait_ge(post_add, 4)
            for par in range(2):
                pool.wait_ge(v_halo[par], 16 * HALO_DMAS * (UNITS // 2))
            pool.memset(g_q, 0.0).then_inc(g_zero, 1)
            layer_norm_rstd(1)
            layer_norm_rstd(2)
            pool.wait_ge(g_upd, TILES)
            zero_blocks()
            steps(pool, 1, body)

        @block.vector
        def _(dve):
            def layer_norm(n):
                for t in range(TILES):
                    last = dve.bn_stats(stats[:, t, :], x_res[:, t, :])
                last.then_inc(ln_stats, 1)
                dve.wait_ge(ln_stats, n + 1)
                for t in range(TILES):
                    last = dve.bn_aggr(mv[:, t, :], stats[:, t, :])
                last.then_inc(ln_mv, 1)
                dve.wait_ge(ln_rstd, 2 * n + 2)
                dve.wait_ge(ln_mv, n + 1)
                for t in range(TILES):
                    done = dve.tensor_scalar(ln_out(n)[:, t * D:(t + 1) * D], x_res[:, t, :], mv[:, t, 0:1],
                                             rstd[:, t:t + 1], ALU.subtract, ALU.mult)
                    if t % 4 == 3:
                        done.then_inc(ln_norm, 1)

            def post(n):
                for g in range(4):
                    dve.wait_ge(post_ps, 4 * n + g + 1)
                    for h, bank in enumerate(post_banks(g)):
                        dst = x_res[:, 4 * g:4 * g + 4, h * HALF:(h + 1) * HALF]
                        last = dve.scalar_tensor_tensor(dst, bank[:, 0:4 * HALF].rearrange("p (t d) -> p t d", t=4),
                                                        0.5, dst, ALU.mult, ALU.add)
                    last.then_inc(post_add, 1)
                dve.wait_ge(post_add, 4 * n + 4)
                for par in range(2):
                    dve.wait_ge(v_halo[par], 16 * HALO_DMAS * (UNITS // 2) * (n + 1))

            def body(st):
                def rotate(n, raw_s, ps_s, sq_s, t1_s, red_s, guard_s):
                    tab = table[st.par(LP)][:, 2 * n * DH:(2 * n + 1) * DH]
                    dve.wait_ge(raw_s, st.count(LP))
                    dve.wait_ge(table_ready, st.count(LP))
                    wait(dve, ps_s, 2 * st.count(LS))
                    dve.tensor_tensor(rot[n].rearrange("p (h d) -> p h d", d=DH),
                                      raw[n].rearrange("p (h d) -> p h d", d=DH),
                                      tab.unsqueeze(1).to_broadcast([P, HEADS, DH]), ALU.mult).then_inc(t1_s, 1)
                    dve.wait_ge(sq_s, st.count(LP))
                    dve.tensor_reduce(ss[:, n * HEADS:(n + 1) * HEADS], square.rearrange("p (h d) -> p h d", d=DH),
                                      AX, ALU.add).then_inc(red_s, 1)
                    dve.wait_ge(red_s, st.count(LP))
                    c = slice(n * HEADS, (n + 1) * HEADS)
                    dve.tensor_scalar(ss[:, c], ss[:, c], 1e-24, None, ALU.max).then_inc(guard_s, 1)

                def normalise(n, add_s, rn_s, rot_s):
                    dve.wait_ge(add_s, st.count(LP))
                    dve.wait_ge(rn_s, st.count(LP))
                    r = rot[n].rearrange("p (h d) -> p h d", d=DH)
                    dve.tensor_tensor(r, r, rn[:, n * HEADS:(n + 1) * HEADS].unsqueeze(2)
                                      .to_broadcast([P, HEADS, DH]), ALU.mult).then_inc(rot_s, 1)

                if st.on(LF):
                    dve.wait_ge(y1t_ps, st.count(LF))
                    t0 = st.tile(LF) * P
                    lo, hi = stream[0:HALF, bass.ds(t0, P)], stream[HALF:P, bass.ds(t0 + 1, P)]
                    dve.tensor_tensor(lo, H[0][0:HALF, 0:P], lo, ALU.add)
                    dve.tensor_tensor(hi, H[0][HALF:P, 0:P], hi, ALU.add).then_inc(attn_res, 1)
                    settled(dve, ln_stats)
                    dve.wait_ge(attn_res, st.count(LF))
                    dve.tensor_copy(xs2, stream[:, bass.ds(t0, P)]).then_inc(xs2_ready, 1)
                if st.on(LP):
                    rotate(0, raw_q, qt_ps, sq_q, t1_q, red_q, guard_q)
                if st.on(LO):
                    dve.wait_ge(av_ps, st.count(LO))
                    dve.wait_ge(rsum_done, st.count(LO))
                    dve.tensor_tensor(o_tok.rearrange("p (h d) -> p h d", d=DH),
                                      S[:].rearrange("p (h d) -> p h d", d=DH),
                                      rsum[st.par(LO)].unsqueeze(2).to_broadcast([P, HEADS, DH]), ALU.mult)\
                       .then_inc(o_ready, 1)
                if st.on(LF):
                    dve.wait_ge(f1_ps, st.count(LF))
                    dve.bn_stats(st1, H[0][:, 0:D]).then_inc(bn_done, 1)
                    settled(dve, ln_stats)
                    dve.wait_ge(bn_done, st.count(LF))
                    dve.bn_aggr(mv1, st1).then_inc(mv_done, 1)
                    dve.wait_ge(mv_done, st.count(LF))
                    wait(dve, rs_done, st.count(LF, 1))
                    dve.tensor_scalar(ve1, mv1[:, 1:2], EPS, None, ALU.add).then_inc(ve_done, 1)
                if st.on(LG) and st.j == 0:
                    n = st.base // 2 + (st.s - LG) // 2 + 1
                    dve.wait_ge(gelu_done, n)
                    wait(dve, ht_ps, st.count(LG, 1))
                    dve.tensor_tensor(hid[:, :, 0:HID], hb[:, :, 0:HID], gelu, ALU.mult).then_inc(hid_done, 1)
                if st.on(LF):
                    dve.wait_ge(rs_done, st.count(LF))
                    dve.tensor_scalar(xn, H[0][:, 0:D], mv1[:, 0:1], rs1, ALU.subtract, ALU.mult)\
                       .then_inc(xn_ready, 1)
                if st.on(LP):
                    rotate(1, raw_k, kt_ps, sq_k, t1_k, red_k, guard_k)
                if st.on(LS):
                    s3 = S[:].rearrange("p (h k) -> p h k", k=SLOTS)
                    dve.wait_ge(scores_ps, st.count(LS))
                    dve.tensor_reduce(smax, s3, AX, ALU.max).then_inc(max_done, 1)
                    dve.wait_ge(max_done, st.count(LS))
                    wait(dve, pt_ps, 2 * st.count(LO))
                    dve.tensor_tensor(prob.rearrange("p (h k) -> p h k", k=SLOTS), s3,
                                      smax.unsqueeze(2).to_broadcast([P, HEADS, SLOTS]), ALU.subtract)\
                       .then_inc(sub_done, 1)
                    for e in range(2):
                        r = slice(e * DH, (e + 1) * DH)
                        last = dve.tensor_scalar(k_bd[r, :, e, 0:WIN], k_bd[r, :, e, P:P + WIN], decay[r, :], None,
                                                 ALU.mult)
                    last.then_inc(halo, 1)
                if st.on(LG):
                    dve.wait_ge(y2t_ps, st.count(LG))
                    t0 = st.tile(LG) * P
                    lo, hi = stream[0:HALF, bass.ds(t0, P)], stream[HALF:P, bass.ds(t0 + 1, P)]
                    bias = bass.ds(st.layer(LG), 1)
                    dve.scalar_tensor_tensor(lo, H[1][0:HALF, 0:P], b2_col[0:HALF, bias], lo, ALU.add, ALU.add)
                    dve.scalar_tensor_tensor(hi, H[1][HALF:P, 0:P], b2_col[HALF:P, bias], hi, ALU.add, ALU.add)\
                       .then_inc(stream_ready, 1)
                if st.on(LX):
                    settled(dve, ln_stats)
                    wait(dve, proj_v, st.count(LX, 2))
                    settled(dve, ln_stats)
                    dve.wait_ge(stream_ready, stream_count(st, LX))
                    dve.tensor_copy(xs[st.par(LX)], stream[:, bass.ds(st.tile(LX) * P, P)]).then_inc(xs_ready, 1)
                if st.on(LP):
                    normalise(0, add_q, rn_q, rot_q)
                if st.on(LS):
                    dve.wait_ge(exp_done, st.count(LS))
                    dve.tensor_reduce(ssum, prob.rearrange("p (h k) -> p h k", k=SLOTS), AX, ALU.add)\
                       .then_inc(sum_done, 1)
                    dve.wait_ge(sum_done, st.count(LS))
                    dve.reciprocal(rsum[st.par(LS)], ssum).then_inc(rsum_done, 1)
                if st.on(LF):
                    dve.wait_ge(h_ps, st.count(LF))
                    b = st.par(LF)
                    off = (st.layer(LF) % 2) * 2 * HID
                    dve.tensor_tensor(hb[:, b, 0:HID], H[0][:, 0:HID], b_1[:, bass.ds(off, HID)], ALU.add)
                    dve.tensor_tensor(hb[:, b, HID:2 * HID], H[1][:, 0:HID], b_1[:, bass.ds(off + HID, HID)], ALU.add)\
                       .then_inc(hb_done, 1)
                if st.on(LP):
                    normalise(1, add_k, rn_k, rot_k)

            def start(n, blk):
                layer_norm(n)
                if blk == 0:
                    dve.wait_ge(const_in, 16 * CONST_DMAS)
                    dve.tensor_copy(mask[:], mask_in)
                    dve.tensor_copy(ident_b[:], ident[:]).then_inc(cast_done, 1)
                for g in range(4):
                    dve.wait_ge(ln_ps, 4 * n + g + 1)
                    dve.tensor_copy(stream[0:HALF, g * 512:g * 512 + 512], T[g % 2][0:HALF, :])
                    dve.tensor_copy(stream[HALF:P, g * 512 + 1:g * 512 + 513], T[g % 2][HALF:P, :])\
                       .then_inc(ln_lo, 1)
                dve.memset(stream[HALF:P, 0:1], 0.0).then_inc(stream_ready, TILES)

            dve.wait_ge(x_in, 64)
            start(0, 0)
            steps(dve, 0, body)
            post(0)

            layer_norm(1)
            dve.wait_ge(g_win, 16 * G_DMAS)
            dve.wait_ge(g_zero, 1)
            for g in range(4):
                cols = slice(g * 512, (g + 1) * 512)
                dve.wait_ge(g_qk_ps, 2 * g + 1)
                for h in range(GH // 2, GH):
                    r = slice(h * GD, (h + 1) * GD)
                    last = dve.tensor_scalar(g_q[r, h, cols], S[r, 0:512], g_bqk[r, 0:1], None, ALU.add)
                last.then_inc(g_q_sb, 1)
                dve.wait_ge(g_qk_ps, 2 * g + 2)
                dve.tensor_scalar(g_k[:, cols], S[:, 512:1024], g_bqk[:, 1:2], None, ALU.add).then_inc(g_k_sb, 1)
            for g in range(4):
                dve.wait_ge(g_v_ps, g + 1)
                dve.tensor_tensor(g_v[:, 4 * g:4 * g + 4, :], H[g % 2][:].rearrange("p (t d) -> p t d", d=D),
                                  g_bv.unsqueeze(1).to_broadcast([P, 4, D]), ALU.add).then_inc(g_v_sb, 1)
            dve.wait_ge(g_zps, 1)
            dve.tensor_scalar(g_dx, H[0][:, 0:TILES], g_b2, None, ALU.add).then_inc(g_zc, 1)
            dve.wait_ge(g_zc, 2)
            dve.tensor_scalar(g_dx, g_dx, 1.0, None, ALU.add).then_inc(g_zc, 1)
            dve.wait_ge(g_zc, 3)
            dve.reciprocal(g_dx, g_dx).then_inc(g_zc, 1)
            dve.wait_ge(g_zc, 4)
            for h in range(GH):
                last = dve.tensor_scalar(g_thr[:, :, h], g_dx, float(L), WINDOWS[h], ALU.mult, ALU.add)
            last.then_inc(g_thr_done, 1)
            dve.wait_ge(g_thr_done, 1)

            chunks_before = [0]

            def mask_row(t, h):
                keys = L - t * P
                dve.tensor_scalar(g_mask[:, 0:keys], g_dist[:, 0:keys], g_thr[:, t, h:h + 1], -BIG,
                                  ALU.is_gt, ALU.mult).then_inc(g_msk, 1)

            def masked_scores(t, h):
                n = t * GH + h
                keys = L - t * P
                dve.wait_ge(g_msk, n + 1)
                if n >= 2:
                    dve.wait_ge(g_tps, tgroups[n - 2][-1][0] + 1)
                nch = (keys + 511) // 512
                for c in range(nch):
                    w = min(512, keys - c * 512)
                    dve.wait_ge(g_sps, chunks_before[0] + c + 1)
                    bank = s_bank(chunks_before[0] + c)
                    last = dve.tensor_tensor_reduce(g_s[n % 2][:, c * 512:c * 512 + w], bank[:, 0:w],
                                                    g_mask[:, c * 512:c * 512 + w], 2.0 / float(L) ** 0.5, -3.0e38,
                                                    ALU.add, ALU.max, g_mx[:, n % 2, c:c + 1])
                    last.then_inc(g_smx, 1)
                chunks_before[0] += nch
                dve.wait_ge(g_smx, chunks_before[0])
                dve.tensor_reduce(g_nm[:, n % 2:n % 2 + 1], g_mx[:, n % 2, 0:nch], AX, ALU.max, negate=True)\
                   .then_inc(g_nmx, 1)

            def evacuate(n, part):
                for gidx, w in tgroups[n][2 * part:2 * part + 2]:
                    if gidx % 2 == 1:
                        wait(dve, g_ops, n - 1)
                        dve.wait_ge(g_tps, gidx + 1)
                        c = gidx - tgroups[n][0][0]
                        dve.tensor_copy(g_pt[n % 2][:, c * 512:c * 512 + w], T[gidx % 2][:, 0:w]).then_inc(g_pt_dve, 1)

            def update(t):
                dve.wait_ge(g_ops2, t + 1)
                dve.wait_ge(g_exp, GH * (t + 1))
                b = t % 2
                dve.reciprocal(g_rs[:, GH * b:GH * b + GH], g_sum[:, GH * b:GH * b + GH]).then_inc(g_rsd, 1)
                dve.wait_ge(g_rsd, t + 1)
                for h in range(GH):
                    c = slice(h * GD, (h + 1) * GD)
                    last = dve.scalar_tensor_tensor(x_res[:, t, c], H[1][:, h * GD:(h + 1) * GD],
                                                    g_rs[:, GH * b + h:GH * b + h + 1], x_res[:, t, c],
                                                    ALU.mult, ALU.add)
                last.then_inc(g_upd, 1)

            UN = TILES * GH
            mask_row(0, 0)
            for n in range(UN + 3):
                if n < UN:
                    masked_scores(n // GH, n % GH)
                if 1 <= n <= UN:
                    evacuate(n - 1, 0)
                    evacuate(n - 1, 1)
                if n + 1 < UN:
                    mask_row((n + 1) // GH, (n + 1) % GH)
                if n >= 6 and (n - 6) % GH == 0:
                    update((n - 6) // GH)
            dve.wait_ge(g_upd, TILES)

            start(2, 1)
            steps(dve, 1, body)
            post(1)

        @block.scalar
        def _(act):
            def body(st):
                if st.on(LO):
                    for n in range(2):
                        act.wait_ge(pt_ps, 2 * st.count(LO) - 1 + n)
                        act.activation(prob_t[:, n * 512:(n + 1) * 512], T[n][:], ACT.Copy).then_inc(pt_sb, 1)
                if st.on(LP):
                    act.wait_ge(proj_q, st.count(LP))
                    wait(act, add_q, st.count(LP, 1))
                    act.activation(raw[0], A[:], ACT.Copy).then_inc(raw_q, 1)
                if st.on(LS):
                    for n in range(2):
                        act.wait_ge(qt_ps, 2 * st.count(LS) - 1 + n)
                        act.activation(q_t[:, n * 512:(n + 1) * 512], T[n][:], ACT.Copy).then_inc(qt_sb, 1)
                if st.on(LP):
                    wait(act, red_k, st.count(LP, 1))
                    act.activation(square, A[:], ACT.Square).then_inc(sq_q, 1)
                if st.on(LG) and st.j == 0:
                    act.wait_ge(hb_done, st.base + st.s - LG + 2)
                    wait(act, hid_done, st.base // 2 + (st.s - LG) // 2)
                    act.activation(gelu, hb[:, :, HID:2 * HID], ACT.Gelu).then_inc(gelu_done, 1)
                if st.on(LS):
                    wait(act, halo, st.count(LS, 1))
                    for n in range(2):
                        act.wait_ge(kt_ps, 2 * st.count(LS) - 1 + n)
                        for e in range(2):
                            r = slice(e * DH, (e + 1) * DH)
                            last = act.activation(k_bd[r, 4 * n:4 * n + 4, e, WIN:WIN + P],
                                                  T[n][r, :].rearrange("p (c t) -> p c t", c=4), ACT.Copy)
                        last.then_inc(kt_sb, 1)
                if st.on(LP):
                    act.wait_ge(proj_k, st.count(LP))
                    wait(act, add_k, st.count(LP, 1))
                    act.activation(raw[1], A[:], ACT.Copy).then_inc(raw_k, 1)
                    act.wait_ge(red_q, st.count(LP))
                    act.activation(square, A[:], ACT.Square).then_inc(sq_k, 1)
                if st.on(LG):
                    act.wait_ge(ht_ps, st.count(LG))
                    act.activation(hid_t, H[1][:, 0:HCH * P], ACT.Copy).then_inc(ht_sb, 1)
                if st.on(LF):
                    act.wait_ge(xnt_ps, st.count(LF))
                    lay = bass.ds(st.layer(LF), 1)
                    act.activation(xn_t, H[0][:, 0:P], ACT.Identity, bias=ln_b[:, lay], scale=ln_g[:, lay])\
                       .then_inc(xnt_sb, 1)
                if st.on(LO):
                    for n in range(2):
                        act.wait_ge(ot_ps, 2 * st.count(LO) - 1 + n)
                        act.activation(o_t[:, n * 512:(n + 1) * 512], T[n][:], ACT.Copy).then_inc(ot_sb, 1)
                if st.on(LG):
                    act.wait_ge(y2_ps, st.count(LG))
                    act.activation(y2, H[1][:, 0:D], ACT.Copy).then_inc(y2_sb, 1)
                if st.on(LS):
                    act.wait_ge(sub_done, st.count(LS))
                    act.activation(prob, prob, ACT.Exp).then_inc(exp_done, 1)
                if st.on(LP):
                    act.wait_ge(proj_v, st.count(LP))
                    wait(act, v_dma[st.par(LP)], 16 * V_DMAS * st.count2(LP, 2))
                    wait(act, v_halo[st.par(LP)], 16 * HALO_DMAS * st.count2(LP, 2))
                    act.activation(v_tok[st.par(LP)].rearrange("p (e c d) -> p c e d", e=2, d=DH),
                                   A[:].rearrange("p (c e d) -> p c e d", e=2, d=DH), ACT.Copy).then_inc(v_ready, 1)
                if st.on(LO):
                    act.wait_ge(y1_ps, st.count(LO))
                    wait(act, y1t_ps, st.count(LO, 1))
                    act.activation(y1, T[0][:, 0:D], ACT.Copy).then_inc(y1_sb, 1)

            steps(act, 0, body)

            for g in range(4):
                act.wait_ge(ln_ps, 4 + g + 1)
                act.activation(g_xt[:, g * 512:(g + 1) * 512], T[g % 2][:], ACT.Copy).then_inc(ln_lo, 1)
            for g in range(4):
                bank = A[:, (g % 2) * 512:(g % 2) * 512 + 512]
                act.wait_ge(g_qin, g + 1)
                act.activation(g_in[:, g * 512:(g + 1) * 512], bank, ACT.Copy).then_inc(g_qin_sb, 1)
                act.activation(g_relu[:, g * 512:(g + 1) * 512], bank, ACT.Relu).then_inc(g_relu_sb, 1)
            act.wait_ge(g_zero, 1)
            act.wait_ge(g_win, 16 * G_DMAS)
            for g in range(4):
                act.wait_ge(g_qk_ps, 2 * g + 1)
                for h in range(GH // 2):
                    r = slice(h * GD, (h + 1) * GD)
                    last = act.activation(g_q[r, h, g * 512:(g + 1) * 512], S[r, 0:512], ACT.Identity,
                                          bias=g_bqk[r, 0:1])
                last.then_inc(g_q_sb, 1)
            for g in range(4):
                act.wait_ge(g_hps, g + 1)
                act.activation(g_h[0:LEARNED, g * 512:(g + 1) * 512],
                               A[0:LEARNED, (g % 2) * 512:(g % 2) * 512 + 512], ACT.Copy).then_inc(g_hsb, 1)
            act.wait_ge(g_zc, 1)
            act.activation(g_dx, g_dx, ACT.Exp, scale=-1.0).then_inc(g_zc, 1)

            UN = TILES * GH

            def evacuate(n, part):
                for gidx, w in tgroups[n][2 * part:2 * part + 2]:
                    if gidx % 2 == 0:
                        wait(act, g_ops, n - 1)
                        act.wait_ge(g_tps, gidx + 1)
                        c = gidx - tgroups[n][0][0]
                        act.activation(g_pt[n % 2][:, c * 512:c * 512 + w], T[0][:, 0:w], ACT.Copy)\
                           .then_inc(g_pt_act, 1)

            for n in range(UN + 3):
                if n >= 6 and (n - 6) % GH == 0:
                    t = (n - 6) // GH
                    act.wait_ge(g_ops, GH * (t + 1))
                    wait(act, g_ops2, t)
                    act.activation(g_ot, H[0][:, 0:P], ACT.Copy).then_inc(g_otsb, 1)
                if 1 <= n <= UN:
                    evacuate(n - 1, 0)
                if n < UN:
                    t, h = n // GH, n % GH
                    act.wait_ge(g_nmx, n + 1)
                    if t >= 2:
                        act.wait_ge(g_rsd, t - 1)
                    act.activation(g_s[n % 2][:, 0:L - t * P], g_s[n % 2][:, 0:L - t * P], ACT.Exp,
                                   bias=g_nm[:, n % 2:n % 2 + 1],
                                   accum_out=g_sum[:, GH * (t % 2) + h:GH * (t % 2) + h + 1]).then_inc(g_exp, 1)
                if 1 <= n <= UN:
                    evacuate(n - 1, 1)

            steps(act, 1, body)

        @block.tensor
        def _(pe):
            def ln_transposes(n):
                if n == 0:
                    pe.wait_ge(const_in, 16 * CONST_DMAS)
                for g in range(4):
                    if g >= 2 or n:
                        wait(pe, ln_lo, 4 * n + g - 1)
                    pe.wait_ge(ln_norm, 4 * n + g + 1)
                    for k in range(4):
                        t = 4 * g + k
                        last = pe.transpose(T[g % 2][:, k * P:(k + 1) * P], ln_out(n)[:, t * D:(t + 1) * D], ident[:])
                    last.then_inc(ln_ps, 1)

            def post(n):
                wait(pe, stream_ready, (n + 1) * STREAM0)
                for g in range(4):
                    if g >= 2 or n:
                        wait(pe, post_add, 4 * n + g - 1)
                    for k in range(4):
                        t = 4 * g + k
                        lo, hi = post_banks(g)
                        pe.transpose(lo[:, k * HALF:(k + 1) * HALF], stream[0:HALF, t * P:(t + 1) * P],
                                     ident[0:HALF, 0:HALF])
                        last = pe.transpose(hi[:, k * HALF:(k + 1) * HALF],
                                            stream[HALF:P, t * P + 1:(t + 1) * P + 1], ident[HALF:P, HALF:P])
                    last.then_inc(post_ps, 1)

            def body(st):
                def weights(lag, per):
                    return (st.layer(lag) % 2) * per

                def transposes(dst, src, s, n):
                    for k in range(4):
                        c = 4 * n + k
                        last = pe.transpose(dst[:, k * P:(k + 1) * P], src[:, c * P:(c + 1) * P], ident[:])
                    last.then_inc(s, 1)

                def project(part, sem_out, free, value):
                    wait(pe, free, value)
                    for n in range(2):
                        off = weights(LP, 3 * INNER) + part * INNER + n * 512
                        last = pe.matmul(A[:, n * 512:(n + 1) * 512], xs[st.par(LP)], w_qkv[:, bass.ds(off, 512)],
                                         start=True, stop=True)
                    last.then_inc(sem_out, 1)

                if st.on(LO):
                    pe.wait_ge(exp_done, st.count(LO))
                    wait(pe, kt_sb, 2 * st.count(LO))
                    wait(pe, y1_sb, st.count(LO, 1))
                    transposes(T[0], prob, pt_ps, 0)
                    transposes(T[1], prob, pt_ps, 1)
                if st.on(LP):
                    pe.wait_ge(xs_ready, st.count(LP))
                    pe.wait_ge(w_in, 16 * W_DMAS * (st.base // UNITS * DEPTH + st.layer(LP) + 1))
                    project(0, proj_q, v_ready, st.count(LP, 1))
                if st.on(LS):
                    pe.wait_ge(rot_q, st.count(LS))
                    for n in range(2):
                        if st.on(LO):
                            pe.wait_ge(pt_sb, 2 * st.count(LO) - 1 + n)
                        else:
                            wait(pe, kt_sb, 2 * st.count(LS, 1))
                        transposes(T[n], rot[0], qt_ps, n)
                if st.on(LF):
                    pe.wait_ge(y1_sb, st.count(LF))
                    wait(pe, hb_done, st.count(LF, 1))
                    pe.transpose(H[0][:, 0:P], y1, ident[:]).then_inc(y1t_ps, 1)
                if st.on(LO):
                    pe.wait_ge(v_dma[st.par(LO)], 16 * V_DMAS * st.count2(LO))
                    wait(pe, v_halo[st.par(LO + 1)], 16 * HALO_DMAS * st.count2(LO, 1))
                    for n in range(2):
                        pe.wait_ge(pt_sb, 2 * st.count(LO) - 1 + n)
                        for c in range(4 * n, 4 * n + 4):
                            for w in range(WINS):
                                v = v_win[st.par(LO)][w].rearrange("p (e c d) -> p c e d", e=2, d=DH)
                                last = pe.matmul(S[w * WIN:(w + 1) * WIN, c * P:(c + 1) * P],
                                                 prob_t[:, c * P + w * WIN:c * P + (w + 1) * WIN], v[:, c],
                                                 start=True, stop=True)
                    last.then_inc(av_ps, 1)
                if st.on(LS):
                    pe.wait_ge(rot_k, st.count(LS))
                    for n in range(2):
                        pe.wait_ge(qt_sb, 2 * st.count(LS) - 1 + n)
                        transposes(T[n], rot[1], kt_ps, n)
                if st.on(LF):
                    pe.wait_ge(xs2_ready, st.count(LF))
                    pe.transpose(H[0][:, 0:P], xs2, ident[:]).then_inc(f1_ps, 1)
                if st.on(LP):
                    project(1, proj_k, sq_q, st.count(LP))
                if st.on(LS):
                    if st.on(LO):
                        pe.wait_ge(o_ready, st.count(LO))
                    for n in range(2):
                        pe.matmul(S[:, n * 512:(n + 1) * 512], ident_b[:],
                                  mask[:, bass.ds(st.tile(LS), 1), :].to_broadcast([P, 8, SLOTS]),
                                  start=True, stop=True)
                    for n in range(2):
                        pe.wait_ge(kt_sb, 2 * st.count(LS) - 1 + n)
                        for c in range(4 * n, 4 * n + 4):
                            for w in range(WINS):
                                last = pe.matmul(S[w * WIN:(w + 1) * WIN, c * P:(c + 1) * P],
                                                 q_t[:, c * P + w * WIN:c * P + (w + 1) * WIN],
                                                 k_bd[:, c, :, w * WIN:w * WIN + SLOTS],
                                                 start=False, stop=True, skip_group_check=True)
                    last.then_inc(scores_ps, 1)
                if st.on(LG):
                    if st.j == 0:
                        pe.wait_ge(hid_done, st.base // 2 + (st.s - LG) // 2 + 1)
                    if st.on(LF):
                        wait(pe, hb_done, st.count(LF, 1))
                    else:
                        wait(pe, hb_done, st.base + UNITS)
                        wait(pe, stream_ready, stream_count(st, LG) + TILES - 1)
                    for c in range(HCH):
                        last = pe.transpose(H[1][:, c * P:(c + 1) * P], hid[:, st.par(LG), c * P:(c + 1) * P], ident[:])
                    last.then_inc(ht_ps, 1)
                if st.on(LF):
                    pe.wait_ge(xn_ready, st.count(LF))
                    pe.transpose(H[0][:, 0:P], xn, ident[:]).then_inc(xnt_ps, 1)
                if st.on(LO):
                    pe.wait_ge(o_ready, st.count(LO))
                    for n in range(2):
                        if st.on(LS):
                            pe.wait_ge(kt_sb, 2 * st.count(LS) - 1 + n)
                        else:
                            pe.wait_ge(pt_sb, 2 * st.count(LO) - 1 + n)
                        transposes(T[n], o_tok, ot_ps, n)
                if st.on(LG):
                    pe.wait_ge(ht_sb, st.count(LG))
                    for c in range(HCH):
                        k = min(P, HID - c * P)
                        off = weights(LG, HCH * D) + c * D
                        last = pe.matmul(H[1][:, 0:D], hid_t[0:k, c * P:(c + 1) * P], w_2[0:k, bass.ds(off, D)],
                                         start=(c == 0), stop=(c == HCH - 1))
                    last.then_inc(y2_ps, 1)
                if st.on(LP):
                    project(2, proj_v, sq_k, st.count(LP))
                if st.on(LG):
                    pe.wait_ge(y2_sb, st.count(LG))
                    pe.transpose(H[1][:, 0:P], y2, ident[:]).then_inc(y2t_ps, 1)
                if st.on(LO):
                    for n in range(2):
                        pe.wait_ge(ot_sb, 2 * st.count(LO) - 1 + n)
                        for c in range(4 * n, 4 * n + 4):
                            off = weights(LO, PAIRS * D) + c * D
                            last = pe.matmul(T[0][:, 0:D], o_t[:, c * P:(c + 1) * P],
                                             w_o[:, bass.ds(off, D)], start=(c == 0), stop=(c == PAIRS - 1))
                    last.then_inc(y1_ps, 1)
                if st.on(LF):
                    pe.wait_ge(xnt_sb, st.count(LF))
                    if st.on(LG):
                        pe.wait_ge(stream_ready, stream_count(st, LG) + TILES)
                    for n in range(2):
                        off = weights(LF, 2 * HID) + n * HID
                        last = pe.matmul(H[n][:, 0:HID], xn_t, w_1[:, bass.ds(off, HID)], start=True, stop=True)
                    last.then_inc(h_ps, 1)

            ln_transposes(0)
            pe.wait_ge(ln_lo, 4)
            pe.wait_ge(cast_done, 1)
            steps(pe, 0, body)
            post(0)

            pe.wait_ge(post_add, 4)
            ln_transposes(1)
            pe.wait_ge(g_win, 16 * G_DMAS)
            for g in range(4):
                pe.wait_ge(ln_lo, 4 + g + 1)
                if g >= 2:
                    pe.wait_ge(g_relu_sb, g - 1)
                pe.matmul(A[:, (g % 2) * 512:(g % 2) * 512 + 512], g_w[:, 0:D], g_xt[:, g * 512:(g + 1) * 512],
                          start=True, stop=True).then_inc(g_qin, 1)
            for g in range(4):
                pe.wait_ge(g_qin_sb, g + 1)
                for c in range(2):
                    wait(pe, (g_q_sb, g_k_sb)[c], (2 - c) * g)
                    pe.matmul(S[:, c * 512:c * 512 + 512], g_w[:, D + c * D:2 * D + c * D],
                              g_in[:, g * 512:(g + 1) * 512], start=True, stop=True).then_inc(g_qk_ps, 1)
            for g in range(4):
                wait(pe, g_v_sb, g - 1)
                for k in range(4):
                    t = 4 * g + k
                    last = pe.matmul(H[g % 2][:, k * D:(k + 1) * D], g_in[:, t * P:(t + 1) * P],
                                     g_w[:, 3 * D:4 * D], start=True, stop=True)
                last.then_inc(g_v_ps, 1)
            for g in range(4):
                pe.wait_ge(g_relu_sb, 4)
                wait(pe, g_hsb, g - 1)
                pe.matmul(A[0:LEARNED, (g % 2) * 512:(g % 2) * 512 + 512], g_w[:, 4 * D:4 * D + LEARNED],
                          g_relu[:, g * 512:(g + 1) * 512], start=True, stop=True).then_inc(g_hps, 1)
            pe.wait_ge(g_hsb, 4)
            pe.wait_ge(g_v_sb, 4)
            for t in range(TILES):
                last = pe.matmul(H[0][:, t:t + 1], g_h[0:LEARNED, t * P:(t + 1) * P],
                                 g_w[0:LEARNED, 4 * D + LEARNED:4 * D + LEARNED + 1], start=True, stop=True)
            last.then_inc(g_zps, 1)
            pe.wait_ge(g_q_sb, 8)
            pe.wait_ge(g_k_sb, 4)

            UN = TILES * GH
            done = [0]

            def transpose_groups(m, part):
                first = tgroups[m][0][0]
                for gidx, w in tgroups[m][2 * part:2 * part + 2]:
                    if gidx >= 2:
                        pe.wait_ge(g_pt_act if gidx % 2 == 0 else g_pt_dve, gidx // 2)
                    c = gidx - first
                    for k in range(w // P):
                        last = pe.transpose(T[gidx % 2][:, k * P:(k + 1) * P],
                                            g_s[m % 2][:, c * 512 + k * P:c * 512 + (k + 1) * P], ident[:])
                    last.then_inc(g_tps, 1)

            for n in range(UN + 3):
                if n < UN:
                    t, h = n // GH, n % GH
                    keys = L - t * P
                    for c in range((keys + 511) // 512):
                        w = min(512, keys - c * 512)
                        if done[0] >= 4:
                            pe.wait_ge(g_smx, done[0] - 3)
                        pe.matmul(s_bank(done[0])[:, 0:w], g_q[:, h, t * P:(t + 1) * P],
                                  g_k[:, t * P + c * 512:t * P + c * 512 + w], start=True, stop=True)\
                          .then_inc(g_sps, 1)
                        done[0] += 1
                if 1 <= n <= UN:
                    pe.wait_ge(g_exp, n)
                    transpose_groups(n - 1, 0)
                if n >= 6 and (n - 6) % GH == 0:
                    t = (n - 6) // GH
                    pe.wait_ge(g_otsb, t + 1)
                    wait(pe, g_upd, t)
                    pe.transpose(H[1][:, 0:P], g_ot, ident[:]).then_inc(g_ops2, 1)
                if 2 <= n <= UN + 1:
                    m = n - 2
                    t, h = m // GH, m % GH
                    nt = TILES - t
                    last_g = tgroups[m][-1][0]
                    pe.wait_ge(g_pt_act, last_g // 2 + 1 if last_g % 2 == 0 else (last_g + 1) // 2)
                    wait(pe, g_pt_dve, (last_g + 1) // 2)
                    if h == 0:
                        if t == 0:
                            pe.wait_ge(g_zc, 1)
                        else:
                            pe.wait_ge(g_otsb, t)
                    for k in range(nt):
                        last = pe.matmul(H[0][h * GD:(h + 1) * GD, 0:P], g_v[:, t + k, h * GD:(h + 1) * GD],
                                         g_pt[m % 2][:, k * P:(k + 1) * P], start=(k == 0), stop=(k == nt - 1))
                    last.then_inc(g_ops, 1)
                if 1 <= n <= UN:
                    transpose_groups(n - 1, 1)
            ln_transposes(2)
            pe.wait_ge(ln_lo, 12)
            steps(pe, 1, body)
            post(1)


def constants():
    import numpy as np

    half = np.arange(0, DH, 2, dtype=np.float32)
    inv_freq = (1.0 / np.power(np.float32(10000.0), half / np.float32(DH))).astype(np.float32)
    t = np.arange(L, dtype=np.float32)
    angle = (t[:, None] * inv_freq[None, :]).astype(np.float64)
    base = (half.astype(np.float64) + 0.4 * DH) / (1.4 * DH)
    power = (np.arange(L) % P - P // 2) / (WIN // 2)
    scale = base[None, :] ** power[:, None]
    cos, sin = np.cos(angle), np.sin(angle)
    rope = np.concatenate([cos * scale, cos * scale, -sin * scale, sin * scale], 1) * QK_SCALE
    rope_k = np.concatenate([cos / scale, cos / scale, -sin / scale, sin / scale], 1)
    rope = np.concatenate([rope, rope_k], 1).astype(np.float32).reshape(TILES, P, 4 * DH).transpose(1, 0, 2)
    decay = np.tile(base ** (P // (WIN // 2)), 4).astype(np.float32)[:, None]
    a, b = np.arange(P)[:, None] % WIN, np.arange(SLOTS)[None, :]
    seen = np.broadcast_to(((b >= a) & (b <= a + WIN))[:, None, :], (P, TILES, SLOTS)).copy()
    seen[0:WIN, 0, 0:WIN] = False
    mask = np.where(seen, 0.0, NEG).astype(np.float32)
    dist = (np.arange(L)[None, :] - np.arange(P)[:, None]).astype(np.float32)
    dist[dist < 0] = 1e9
    eye = np.eye(P, dtype=np.float32)
    return {"c_rope": np.ascontiguousarray(rope), "c_decay": decay, "c_mask": mask, "c_ident": eye, "c_dist": dist}


def kernel(**inputs):
    import numpy as np
    import concourse.bacc as bacc
    from concourse.bass_utils import run_bass_kernel_spmd

    a = {k: np.asarray(v) for k, v in inputs.items()}
    w2 = a["L0_ffn_W2"]
    w2 = np.concatenate([w2, np.zeros((DEPTH, HCH * P - HID, D), w2.dtype)], 1)
    b = a["L0_attn_bqkv"]
    arrays = {
        "x": a["L0_attn_x"], "fWqkv": a["L0_ffn_Wqkv"], "fqs": a["L0_ffn_q_scale"], "fks": a["L0_ffn_k_scale"],
        "fWo": a["L0_ffn_Wo"], "fg": a["L0_ffn_ln_g"].T, "fb": a["L0_ffn_ln_b"].T, "fW1": a["L0_ffn_W1"],
        "fb1": a["L0_ffn_b1"], "fW2": w2.reshape(DEPTH, HCH, P, D).transpose(0, 2, 1, 3), "fb2": a["L0_ffn_b2"].T,
        "aWqT": a["L0_attn_Wq"].T, "aWqkvT": a["L0_attn_Wqkv"].T, "abqkT": b[0:2 * D].reshape(2, D).T,
        "abv": b[2 * D:3 * D], "aWopT": a["L0_attn_Wop"].T, "aW2T": a["L0_attn_W2"].T, "ab2": a["L0_attn_b2"],
    }
    arrays.update(constants())
    arrays = {k: np.ascontiguousarray(v) for k, v in arrays.items()}
    nc = bacc.Bacc("TRN2", target_bir_lowering=False, num_devices=1)
    args = {k: nc.dram_tensor(k, v.shape, mybir.dt.from_np(v.dtype), kind="ExternalInput").ap()
            for k, v in arrays.items()}
    out = nc.dram_tensor("out", (1, L, D), F32, kind="ExternalOutput").ap()
    build(nc, out=out, **args)
    r = run_bass_kernel_spmd(nc, [arrays], core_ids=[0])
    return r.results[0]["out"]
```
